# Optimizing a Trainium2 kernel written in Bass

```python
import numpy as np
import jax
import jax.numpy as jnp

def _softmax(x, axis=-1):
    return jax.nn.softmax(x, axis=axis)

def _gelu(x):
    return jax.nn.gelu(x, approximate=True)

def _silu(x):
    return jax.nn.silu(x)

def _sigmoid(x):
    return jax.nn.sigmoid(x)

def _layernorm(x, axis=-1, eps=1e-05):
    m = jnp.mean(x, axis=axis, keepdims=True)
    v = jnp.var(x, axis=axis, keepdims=True)
    return (x - m) / jnp.sqrt(v + eps)

def _scatter_add(tgt, idx, src, axis=0):
    return tgt.at[idx].add(src)

def _segment_sum(src, seg, n):
    return jax.ops.segment_sum(src, seg, n)
kernel_name = 'mk_gnn_preln_d1_gnn_r8_d8cb73'

def setup_inputs(seed: int=0):
    np.random.seed(seed)
    _w = jnp.asarray

    def _rec_inputs():
        import jax
        import jax.numpy as jnp
        _gk = jax.random.key(seed)
        x = -0.0001006 + 1 * jax.random.normal(jax.random.fold_in(_gk, 1), (12500, 48), jnp.float32)
        src = jax.random.randint(jax.random.fold_in(_gk, 2), (400000,), 0, 12500, jnp.int32)
        dst = jnp.minimum((12500 * jax.random.uniform(jax.random.fold_in(_gk, 3), (400000,)) ** 2.0).astype(jnp.int32), 99999)
        _o = jnp.argsort(dst, stable=True)
        src = src[_o]
        dst = dst[_o]
        edge_attr_32 = 0.000189758 + 1.00013 * jax.random.normal(jax.random.fold_in(_gk, 11), (400000, 32), jnp.float32)
        return (x, src, dst, edge_attr_32)
    x, src, dst, edge_attr_32 = _rec_inputs()

    def _L0_gnn_setup():
        import jax, jax.numpy as jnp
        import numpy as np
        N_NODES = 12500
        key = jax.random.key(seed)
        k1, k2, k3, k4, k5, k6 = jax.random.split(key, 6)
        node_dim, edge_dim, hidden = (48, 32, 128)
        E = 200000
        x = jax.random.normal(k1, (N_NODES, node_dim), dtype=jnp.float32)
        edge_index = jax.random.randint(k2, (2, E), 0, N_NODES, dtype=jnp.int64)
        edge_attr = jax.random.normal(k3, (E, edge_dim), dtype=jnp.float32)
        in_dim = 2 * node_dim + edge_dim
        s1 = 1.0 / np.sqrt(in_dim)
        s2 = 1.0 / np.sqrt(hidden)
        W1 = jax.random.uniform(k4, (in_dim, hidden), minval=-s1, maxval=s1, dtype=jnp.float32)
        b1 = jax.random.uniform(k5, (hidden,), minval=-s1, maxval=s1, dtype=jnp.float32)
        W2 = jax.random.uniform(k6, (hidden, node_dim), minval=-s2, maxval=s2, dtype=jnp.float32)
        b2 = jnp.zeros((node_dim,), dtype=jnp.float32)
        return {'x': x, 'edge_index': edge_index, 'edge_attr': edge_attr, 'W1': W1, 'b1': b1, 'W2': W2, 'b2': b2}
    _L0_gnn_all = _L0_gnn_setup()
    _L0_gnn_in = {k: v for k, v in _L0_gnn_all.items() if k in ('W1', 'b1', 'W2', 'b2')}
    del _L0_gnn_all
    return {'x': x, 'src': src, 'dst': dst, 'edge_attr_32': edge_attr_32, 'L0_gnn_W1': _L0_gnn_in['W1'], 'L0_gnn_b1': _L0_gnn_in['b1'], 'L0_gnn_W2': _L0_gnn_in['W2'], 'L0_gnn_b2': _L0_gnn_in['b2']}

def reference(x, src, dst, edge_attr_32, L0_gnn_W1, L0_gnn_b1, L0_gnn_W2, L0_gnn_b2):
    import jax
    import jax.numpy as jnp

    def _L0_gnn_ref(x, edge_index, edge_attr, W1, b1, W2, b2):
        import jax, jax.numpy as jnp
        import numpy as np
        N_NODES = 12500
        src, dst = (edge_index[0], edge_index[1])
        x_i = x[dst]
        x_j = x[src]
        tmp = jnp.concatenate([x_i, x_j, edge_attr], axis=1)
        h = jax.nn.relu(tmp @ W1 + b1)
        msg = h @ W2 + b2
        out = jax.ops.segment_sum(msg, dst, num_segments=N_NODES)
        return out
    edge_index = jnp.stack([src, dst])
    h = jnp.maximum(_layernorm(x, axis=-1), 0.0)
    x = x + _L0_gnn_ref(h, edge_index, edge_attr_32, L0_gnn_W1, L0_gnn_b1, L0_gnn_W2, L0_gnn_b2)
    return x

_drawn_inputs = setup_inputs


def setup_inputs(seed=0):
    import zlib

    import numpy as np

    out = dict(_drawn_inputs(seed))
    spreads = {'L0_gnn_b2': (0.0, 0.1)}
    factors = {}
    for name, (base, spread) in spreads.items():
        noise = np.random.default_rng([zlib.crc32(name.encode()), seed]).standard_normal(out[name].shape)
        drawn = base * np.exp(spread * noise) if base else spread * noise
        out[name] = jnp.asarray(drawn.astype(out[name].dtype))
    for name, factor in factors.items():
        out[name] = (out[name] * factor).astype(out[name].dtype)
    return out
```

```python
from contextlib import ExitStack

import concourse.bass as bass
from concourse import mybir

F32 = mybir.dt.float32
I32 = mybir.dt.int32
ALU = mybir.AluOpType
ACT = mybir.ActivationFunctionType
AX = mybir.AxisListType
ds = bass.ds

P = 128
BANK = 512
TILES = 5
SLOTS = 5
WIN = 64
EPS = 1e-5


def gnn(nc, x, x_t, src_t, dst_t, edge_t, w1, b1, w2, b2, out_t):
    n_nodes, feat = x.shape
    edge_feat, n_edges = edge_t.shape
    hidden = w1.shape[1]
    n_tiles = n_edges // P
    groups = n_tiles // TILES
    bodies = groups // SLOTS
    per_part = n_nodes // P
    main_nodes = per_part * P
    tail = n_nodes - main_nodes
    cols = per_part + 1
    chunk_cols, units = 14, 7
    chunks = cols // chunk_cols
    e_cols = TILES * P
    e_row = WIN
    k_rows = WIN + edge_feat
    fin_cols = 500
    fin_steps = n_nodes // fin_cols
    gen_cols, gen_k = 250, 5
    rounds = n_nodes // (gen_cols * gen_k)
    assert hidden == P and tail > 0 and chunks * chunk_cols == cols and chunk_cols == 2 * units
    assert n_tiles * P == n_edges and bodies * SLOTS * TILES == n_tiles and bodies >= 2
    assert fin_steps * fin_cols == n_nodes and rounds * gen_cols * gen_k == n_nodes
    assert fin_steps % SLOTS == 0

    a_table = nc.dram_tensor("a_table", [n_nodes, hidden], F32).ap()
    b_table = nc.dram_tensor("b_table", [n_nodes, hidden], F32).ap()

    ctx = ExitStack()
    with ctx:
        def sb(name, shape, dt=F32):
            return ctx.enter_context(nc.sbuf_tensor(name, shape, dt))

        def sem(name):
            return ctx.enter_context(nc.semaphore(name))

        acc = sb("acc", [P, n_nodes])
        cnt = sb("cnt", [1, n_nodes])
        src_sb = sb("src_sb", [P, n_tiles], I32)
        dst_sb = sb("dst_sb", [P, n_tiles], I32)
        dst_rel = sb("dst_rel", [P, n_tiles])
        gath = sb("gath", [P, SLOTS, TILES, hidden])
        lhs = sb("lhs", [k_rows, SLOTS, e_cols])
        rhs = sb("rhs", [k_rows, SLOTS, hidden])
        onehot = sb("onehot", [P, SLOTS, TILES, WIN])
        idx = sb("idx", [P, SLOTS, TILES], I32)
        h_sb = sb("h_sb", [P, chunk_cols, feat])
        sq_sb = sb("sq_sb", [P, chunk_cols, feat])
        h_t = sb("h_t", [feat, units, 2 * P])
        b_stage = sb("b_stage", [P, units, 2, hidden])
        a_stage = sb("a_stage", [P, units, 2, hidden])
        w_ba = sb("w_ba", [feat, 2 * hidden])
        b1_bc = sb("b1_bc", [P, hidden])
        w2_sb = sb("w2_sb", [hidden, P])
        b2_sb = sb("b2_sb", [1, P])
        ident = sb("ident", [P, P])
        ones_row = sb("ones_row", [1, P])
        ones_col = sb("ones_col", [P, 1])
        iota_gen = sb("iota_gen", [P, gen_cols])
        base_f = sb("base_f", [1, groups])
        base_i = sb("base_i", [1, groups], I32)
        stat = sb("stat", [P, 6, chunk_cols])
        covered = sb("covered", [P, 1])
        flag = sb("flag", [1, 1], I32)
        gen_idx = sb("gen_idx", [P, 2], I32)
        gen_dst = sb("gen_dst", [P, 2])
        gen_rel = sb("gen_rel", [P, gen_k])
        gen_off = sb("gen_off", [P, gen_k])

        x_sb = acc[:, 0:cols * feat].rearrange("p (j f) -> p j f", f=feat)
        inside = dst_sb[:].bitcast(F32)
        fin_x = gath[0:feat].rearrange("p s t h -> p s (t h)")
        fin_o = lhs[0:feat]
        gen_z = gath[:, 0, 0, :]
        gen_b = gath[:, 1, 0, :]
        gen_a = gath[:, 2, 0, :]
        gen_oh = onehot[:, 0:4].rearrange("p s t w -> p (s t w)")[:, 0:gen_k * gen_cols]
        gen_oh3 = gen_oh.rearrange("p (k n) -> p k n", n=gen_cols)

        ps = ctx.enter_context(nc.psum_tensor("ps", [P, 8, BANK], F32))
        ps_b = ps[:, 0:3, 0:2 * hidden].rearrange("p s (j w) -> p s j w", j=2)
        ps_a = ps[:, 3:6, 0:2 * hidden].rearrange("p s (j w) -> p s j w", j=2)
        ps_ht = ps[0:feat, 6:8, 0:2 * P]
        ps_z = ps[:, 0:4, :].rearrange("p (s b) c -> p s (b c)", b=2)[:, :, 0:e_cols]
        ps_oht = ps[0:WIN, 4:6, :].rearrange("p b c -> p (b c)")[:, 0:e_cols]
        ps_base = ps[:, 6:8, :]
        ps_sum = ps[:, 6, 0:WIN]
        ps_cnt = ps[0:1, 6, WIN:2 * WIN]
        iota_ps = ps[:, 7, 0:WIN]

        x_first, x_rest, x_tail = sem("x_first"), sem("x_rest"), sem("x_tail")
        w_in, b1_in, we_in, last_w_in = sem("w_in"), sem("b1_in"), sem("we_in"), sem("last_w_in")
        dst_in, src_in = sem("dst_in"), sem("src_in")
        w2_zero = sem("w2_zero")
        tail_zero, ident_zero, ident_ready, zeroed = sem("tail_zero"), sem("ident_zero"), sem("ident_ready"), sem("zeroed")
        ones_ready, iota_ready, iota_copied = sem("ones_ready"), sem("iota_ready"), sem("iota_copied")
        base_ready, base_spread, rel_ready, inside_step = sem("base_ready"), sem("base_spread"), sem("rel_ready"), sem("inside_step")
        stat_step, var_ready, std_ready, rstd_ready = sem("stat_step"), sem("var_ready"), sem("std_ready"), sem("rstd_ready")
        h_ready, h_turned, ht_ready, prod_ready = sem("h_ready"), sem("h_turned"), sem("ht_ready"), sem("prod_ready")
        b_ready, a_ready = sem("b_ready"), sem("a_ready")
        b_stored = [sem(f"b_stored{u}") for u in range(units)]
        a_stored = [sem(f"a_stored{u}") for u in range(units)]
        idx_ready, hot_ready, hot_turned, lhs_ready = sem("idx_ready"), sem("hot_ready"), sem("hot_turned"), sem("lhs_ready")
        gathered = [sem(f"gathered{u}") for u in range(SLOTS)]
        loaded = [sem(f"loaded{u}") for u in range(SLOTS)]
        z_ready, z_added, r_ready, summed, acc_done = sem("z_ready"), sem("z_added"), sem("r_ready"), sem("summed"), sem("acc_done")
        cov_summed, flag_ready = sem("cov_summed"), sem("flag_ready")
        g_idx_in, g_e_in, g_gathered = sem("g_idx_in"), sem("g_e_in"), sem("g_gathered")
        g_z, g_step, g_r, g_hot, g_sum, g_acc = sem("g_z"), sem("g_step"), sem("g_r"), sem("g_hot"), sem("g_sum"), sem("g_acc")
        sums_complete = sem("sums_complete")
        fin_in = [sem(f"fin_in{u}") for u in range(SLOTS)]
        fin_prod, fin_ready = sem("fin_prod"), sem("fin_ready")
        fin_stored = [sem(f"fin_stored{u}") for u in range(SLOTS)]

        b_main = b_table[0:main_nodes, :].rearrange("(p j) h -> p j h", j=per_part)
        a_main = a_table[0:main_nodes, :].rearrange("(p j) h -> p j h", j=per_part)
        x_main = x[0:main_nodes, :].rearrange("(p j) f -> p j f", j=per_part)

        prod_slot = (0, 1, 2, 0, 1, 2, 1)
        prod_gap = (4, 2, 4, 3, 3, 3, 2)

        waited = sem("waited")

        block = ctx.enter_context(nc.Block())

        @block.sync
        def _(sp):
            sp.dma_start(x_sb[:, 0:chunk_cols, :], x_main[:, 0:chunk_cols, :]).then_inc(x_first, 16)
            sp.dma_start(w_ba[:, 0:hidden], w1[feat:2 * feat, :]).then_inc(w_in, 16)
            sp.dma_start(w_ba[:, hidden:2 * hidden], w1[0:feat, :]).then_inc(w_in, 16)
            sp.dma_start(x_sb[:, chunk_cols:per_part, :], x_main[:, chunk_cols:per_part, :]).then_inc(x_rest, 16)
            sp.wait_ge(tail_zero, 1)
            sp.dma_start(x_sb[0:tail, per_part, :], x[main_nodes:n_nodes, :]).then_inc(x_tail, 16)
            sp.dma_start(b1_bc[:], b1.partition_broadcast(P)).then_inc(b1_in, 16)
            sp.dma_start(dst_sb[:], dst_t).then_inc(dst_in, 16)
            sp.dma_start(src_sb[:], src_t).then_inc(src_in, 16)
            for s in range(SLOTS):
                sp.dma_start(rhs[e_row:k_rows, s, :], w1[2 * feat:2 * feat + edge_feat, :]).then_inc(we_in, 16)
            sp.wait_ge(w2_zero, 2)
            sp.dma_start(w2_sb[:, 0:feat], w2).then_inc(last_w_in, 16)
            sp.dma_start(b2_sb[:, 0:feat], b2).then_inc(last_w_in, 16)

            def store_chunk(c, last):
                for u in range(units):
                    j = c * chunk_cols + 2 * u
                    sp.wait_ge(b_ready, c * units + u + 1)
                    if last and u == units - 1:
                        sp.dma_start(b_main[:, j, :], b_stage[:, u, 0, :]).then_inc(b_stored[u], 16)
                        sp.dma_start(b_table[main_nodes:n_nodes, :], b_stage[0:tail, u, 1, :]).then_inc(b_stored[u], 16)
                    else:
                        sp.dma_start(b_main[:, ds(j, 2), :], b_stage[:, u, :, :]).then_inc(b_stored[u], 16)
                    sp.wait_ge(a_ready, c * units + u + 1)
                    if last and u == units - 1:
                        sp.dma_start(a_main[:, j, :], a_stage[:, u, 0, :]).then_inc(a_stored[u], 16)
                        sp.dma_start(a_table[main_nodes:n_nodes, :], a_stage[0:tail, u, 1, :]).then_inc(a_stored[u], 16)
                    else:
                        sp.dma_start(a_main[:, ds(j, 2), :], a_stage[:, u, :, :]).then_inc(a_stored[u], 16)

            with sp.Fori(0, chunks - 1) as c:
                store_chunk(c, False)
            store_chunk(chunks - 1, True)

            sp.wait_ge(base_ready, 2)
            for u in range(units):
                sp.wait_ge(a_stored[u], 16 * (chunks + (u == units - 1)))

            def load_group(s, u, first):
                if not first:
                    sp.wait_ge(z_ready, s - SLOTS + 1)
                sp.dma_start(lhs[e_row:k_rows, u, :], edge_t[:, ds(s * e_cols, e_cols)]).then_inc(loaded[u], 16)
                base = sp.value_load(base_i[0:1, ds(s, 1)], min_val=0, max_val=n_nodes - WIN)
                sp.dma_start(rhs[0:WIN, u, :], a_table[ds(base, WIN), :]).then_inc(loaded[u], 16)

            for u in range(SLOTS):
                load_group(u, u, True)
            with sp.Fori(1, bodies) as it:
                for u in range(SLOTS):
                    load_group(it * SLOTS + u, u, False)

            sp.wait_ge(flag_ready, 1)
            outside = sp.value_load(flag[0:1, 0:1], min_val=0, max_val=n_edges)
            with sp.If(outside > 0):
                def load_tile(t):
                    sp.dma_start(gen_idx[:, 0:1], src_t[:, ds(t, 1)], allow_slow_non_contiguous=True).then_inc(g_idx_in, 16)
                    sp.dma_start(gen_idx[:, 1:2], dst_t[:, ds(t, 1)], allow_slow_non_contiguous=True).then_inc(g_idx_in, 16)
                    sp.dma_start(lhs[e_row:k_rows, 1, 0:P], edge_t[:, ds(t * P, P)]).then_inc(g_e_in, 16)

                load_tile(0)
                with sp.Fori(1, n_tiles) as t:
                    sp.wait_ge(g_acc, t * rounds)
                    sp.sem_inc(waited)
                    load_tile(t)
            with sp.Else():
                sp.nop()

            def load_x(n, u):
                sp.dma_start(fin_x[:, u, 0:fin_cols], x_t[:, ds(n * fin_cols, fin_cols)]).then_inc(fin_in[u], 16)

            def store_out(n, u):
                sp.wait_ge(fin_ready, n + 1)
                sp.dma_start(out_t[:, ds(n * fin_cols, fin_cols)], fin_o[:, u, 0:fin_cols]).then_inc(fin_stored[u], 16)

            sp.wait_ge(sums_complete, 1)
            for u in range(SLOTS):
                load_x(u, u)
            with sp.Fori(0, fin_steps // SLOTS - 1) as it:
                for u in range(SLOTS):
                    store_out(it * SLOTS + u, u)
                    load_x((it + 1) * SLOTS + u, u)
            for u in range(SLOTS):
                store_out(fin_steps - SLOTS + u, u)
            for u in range(SLOTS):
                sp.wait_ge(fin_stored[u], 16 * (fin_steps // SLOTS))

        @block.gpsimd
        def _(pool):
            nc.gpsimd.memset(x_sb[:, per_part, :], 0.0).then_inc(tail_zero, 1)
            nc.gpsimd.memset(ident[:], 0.0).then_inc(ident_zero, 1)
            nc.gpsimd.memset(w2_sb[:], 0.0).then_inc(w2_zero, 1)
            nc.gpsimd.memset(b2_sb[:], 0.0).then_inc(w2_zero, 1)
            pool.wait_ge(ident_zero, 1)
            nc.gpsimd.affine_select(out=ident[:], in_=ident[:], compare_op=ALU.not_equal, fill=1.0, base=0,
                                    pattern=[[-1, P]], channel_multiplier=1).then_inc(ident_ready, 1)
            nc.gpsimd.memset(ones_row[:], 1.0).then_inc(ones_ready, 1)
            nc.gpsimd.memset(ones_col[:], 1.0).then_inc(ones_ready, 1)
            nc.gpsimd.iota(iota_gen[:], [[1, gen_cols]], base=0, channel_multiplier=0,
                           allow_small_or_imprecise_dtypes=True).then_inc(iota_ready, 1)
            nc.gpsimd.iota(gen_off[:], [[gen_cols, gen_k]], base=0, channel_multiplier=0,
                           allow_small_or_imprecise_dtypes=True).then_inc(iota_ready, 1)
            nc.gpsimd.memset(cnt[:], 0.0).then_inc(zeroed, 1)
            pool.wait_ge(h_ready, chunks)
            nc.gpsimd.memset(acc[:], 0.0).then_inc(zeroed, 1)

            for u in range(units):
                pool.wait_ge(b_stored[u], 16 * (chunks + (u == units - 1)))

            def gather_group(s, u):
                pool.wait_ge(idx_ready, s + 1)
                pool.sem_inc(waited)
                for t in range(TILES):
                    pool.indirect_dma_start(
                        gath[:, u, t, :], None, b_table,
                        bass.IndirectOffsetOnAxis(ap=idx[:, u, t:t + 1], axis=0)).then_inc(gathered[u], 16)

            for u in range(SLOTS):
                gather_group(u, u)
            with pool.Fori(1, bodies) as it:
                for u in range(SLOTS):
                    gather_group(it * SLOTS + u, u)

            pool.wait_ge(flag_ready, 1)
            outside = pool.value_load(flag[0:1, 0:1], min_val=0, max_val=n_edges)
            with pool.If(outside > 0):
                with pool.Fori(0, n_tiles) as t:
                    pool.wait_ge(g_idx_in, 32 * (t + 1))
                    pool.sem_inc(waited)
                    pool.indirect_dma_start(gen_b, None, b_table, bass.IndirectOffsetOnAxis(
                        ap=gen_idx[:, 0:1], axis=0)).then_inc(g_gathered, 16)
                    pool.indirect_dma_start(gen_a, None, a_table, bass.IndirectOffsetOnAxis(
                        ap=gen_idx[:, 1:2], axis=0)).then_inc(g_gathered, 16)
            with pool.Else():
                pool.nop()

        @block.scalar
        def _(act):
            def root(c):
                act.wait_ge(var_ready, c + 1)
                nc.scalar.activation(stat[:, 3, :], stat[:, 2, :], ACT.Sqrt).then_inc(std_ready, 1)

            def take_ht(c, u):
                act.wait_ge(h_turned, c * units + u + 1)
                nc.scalar.copy(h_t[:, u, :], ps_ht[:, u % 2, :]).then_inc(ht_ready, 1)

            def take_b(c, u, first):
                act.wait_ge(prod_ready, c * units + u + 1)
                if not first:
                    act.wait_ge(b_stored[u], 16 * c)
                nc.scalar.copy(b_stage[:, u, :, :], ps_b[:, prod_slot[u], :, :]).then_inc(b_ready, 1)

            root(0)
            for u in range(units):
                take_ht(0, u)
            root(1)

            def chunk(c, first, ht, stats):
                for u in range(units):
                    take_b(c, u, first)
                    if ht:
                        take_ht(c + 1, u)
                    if stats and u == 3:
                        root(c + 2)

            chunk(0, True, True, True)
            with act.Fori(1, chunks - 2) as c:
                chunk(c, False, True, True)
            chunk(chunks - 2, False, True, False)
            act.wait_ge(src_in, 16)

            def take_idx(s, u, first):
                if not first:
                    act.wait_ge(summed, s - SLOTS + 1)
                nc.scalar.copy(idx[:, u, :], src_sb[:, ds(s * TILES, TILES)]).then_inc(idx_ready, 1)

            take_idx(0, 0, True)
            take_idx(1, 1, True)
            chunk(chunks - 1, False, False, False)
            act.wait_ge(iota_ready, 2)
            act.wait_ge(rel_ready, 2)
            nc.scalar.copy(iota_ps, iota_gen[:, 0:WIN]).then_inc(iota_copied, 1)

            def take_hot(s, u, first):
                act.wait_ge(hot_turned, s + 1)
                if not first:
                    act.wait_ge(z_ready, s - SLOTS + 1)
                nc.scalar.copy(lhs[0:WIN, u, :], ps_oht).then_inc(lhs_ready, 1)

            def rectify(s, u):
                act.wait_ge(z_added, s + 1)
                z = gath[:, u, :, :]
                nc.scalar.activation(z, z, ACT.Relu).then_inc(r_ready, 1)

            for s in range(SLOTS):
                if s >= 2:
                    take_idx(s, s, True)
                take_hot(s, s, True)
                if s >= 2:
                    rectify(s - 2, s - 2)
            with act.Fori(1, bodies) as it:
                for u in range(SLOTS):
                    s = it * SLOTS + u
                    take_idx(s, u, False)
                    take_hot(s, u, False)
                    rectify(s - 2, (u - 2) % SLOTS)
            rectify(groups - 2, SLOTS - 2)
            rectify(groups - 1, SLOTS - 1)

            act.wait_ge(flag_ready, 1)
            outside = act.value_load(flag[0:1, 0:1], min_val=0, max_val=n_edges)
            with act.If(outside > 0):
                with act.Fori(0, n_tiles) as t:
                    act.wait_ge(g_step, 4 * t + 4)
                    nc.scalar.activation(gen_z, gen_z, ACT.Relu).then_inc(g_r, 1)
            with act.Else():
                act.nop()

        @block.vector
        def _(dve):
            def stats(c, chained):
                xc = x_sb[:, ds(c * chunk_cols, chunk_cols), :]
                nc.vector.tensor_reduce(stat[:, 0, :], xc, AX.X, ALU.add).then_inc(stat_step, 1)
                dve.wait_ge(stat_step, 4 * c + 1)
                nc.vector.scalar_tensor_tensor(
                    xc, stat[:, 0, :].unsqueeze(2).to_broadcast([P, chunk_cols, feat]), -1.0 / feat, xc,
                    ALU.mult, ALU.add).then_inc(stat_step, 1)
                dve.wait_ge(stat_step, 4 * c + 2)
                nc.vector.tensor_tensor(sq_sb[:], xc, xc, ALU.mult).then_inc(stat_step, 1)
                dve.wait_ge(stat_step, 4 * c + 3)
                nc.vector.tensor_reduce(stat[:, 1, :], sq_sb[:], AX.X, ALU.add).then_inc(stat_step, 1)
                dve.wait_ge(stat_step, 4 * c + 4)
                nc.vector.tensor_scalar(stat[:, 2, :], stat[:, 1, :], 1.0 / feat, EPS, ALU.mult, ALU.add
                                        ).then_inc(var_ready, 1)
                dve.wait_ge(std_ready, c + 1)
                if chained:
                    dve.wait_ge(h_ready, c)
                nc.vector.reciprocal(stat[:, 4, :], stat[:, 3, :]).then_inc(rstd_ready, 1)

            def write_h(c, first):
                dve.wait_ge(rstd_ready, c + 1)
                if not first:
                    dve.wait_ge(h_turned, c * units)
                nc.vector.scalar_tensor_tensor(
                    h_sb[:], x_sb[:, ds(c * chunk_cols, chunk_cols), :], 0.0,
                    stat[:, 4, :].unsqueeze(2).to_broadcast([P, chunk_cols, feat]),
                    ALU.max, ALU.mult).then_inc(h_ready, 1)

            def take_a(c, u, first):
                dve.wait_ge(prod_ready, c * units + u + 1)
                if not first:
                    dve.wait_ge(a_stored[u], 16 * c)
                nc.vector.tensor_tensor(
                    a_stage[:, u, :, :], ps_a[:, prod_slot[u], :, :],
                    b1_bc[:].unsqueeze(1).to_broadcast([P, 2, hidden]), ALU.add).then_inc(a_ready, 1)

            def chunk(c, first, h, more):
                if h:
                    write_h(c + 1, False)
                for u in range(units):
                    take_a(c, u, first)
                    if more and u == 3:
                        stats(c + 2, True)

            dve.wait_ge(x_first, 16)
            stats(0, False)
            write_h(0, True)
            dve.wait_ge(x_rest, 16)
            dve.wait_ge(x_tail, 16)
            stats(1, True)
            dve.wait_ge(b1_in, 16)
            chunk(0, True, True, True)
            with dve.Fori(1, chunks - 2) as c:
                chunk(c, False, True, True)
            dve.wait_ge(dst_in, 16)
            firsts = dst_sb[0:1, :].rearrange("p (g t) -> p g t", t=TILES)[:, :, 0]
            nc.vector.tensor_scalar(base_f[:], firsts, float(n_nodes - WIN), None, ALU.min).then_inc(base_ready, 1)
            nc.vector.tensor_scalar(base_i[:], firsts, float(n_nodes - WIN), None, ALU.min).then_inc(base_ready, 1)
            chunk(chunks - 2, False, True, False)
            chunk(chunks - 1, False, False, False)
            dve.wait_ge(base_spread, 1)
            half = (groups + 1) // 2
            for k in range(2):
                g0, g1 = k * half, min(groups, (k + 1) * half)
                nc.vector.tensor_tensor(
                    dst_rel[:, g0 * TILES:g1 * TILES].rearrange("p (g t) -> p g t", t=TILES),
                    dst_sb[:, g0 * TILES:g1 * TILES].rearrange("p (g t) -> p g t", t=TILES),
                    ps_base[:, k, 0:g1 - g0].unsqueeze(2).to_broadcast([P, g1 - g0, TILES]),
                    ALU.subtract).then_inc(rel_ready, 1)

            dve.wait_ge(rel_ready, 2)
            nc.vector.tensor_scalar(inside, dst_rel[:], 0.0, None, ALU.is_ge).then_inc(inside_step, 1)
            dve.wait_ge(inside_step, 1)
            nc.vector.scalar_tensor_tensor(inside, dst_rel[:], float(WIN), inside, ALU.is_lt, ALU.mult,
                                           accum_out=covered[:]).then_inc(inside_step, 1)
            dve.wait_ge(zeroed, 2)
            dve.wait_ge(iota_copied, 1)

            def make_hot(s, u, first):
                if not first:
                    dve.wait_ge(summed, s - SLOTS + 1)
                nc.vector.tensor_tensor(
                    onehot[:, u, :, :], iota_ps.unsqueeze(1).to_broadcast([P, TILES, WIN]),
                    dst_rel[:, ds(s * TILES, TILES)].unsqueeze(2).to_broadcast([P, TILES, WIN]),
                    ALU.is_equal).then_inc(hot_ready, 1)

            def add_z(s, u, fills):
                dve.wait_ge(z_ready, s + 1)
                dve.wait_ge(gathered[u], 16 * TILES * fills)
                z = gath[:, u, :, :].rearrange("p t h -> p (t h)")
                nc.vector.tensor_tensor(z, ps_z[:, u % 2, :], z, ALU.add).then_inc(z_added, 1)

            def accumulate(s, u, first):
                base = dve.value_load(base_i[0:1, ds(s, 1)], min_val=0, max_val=n_nodes - WIN)
                dve.wait_ge(summed, s + 1)
                if not first:
                    dve.wait_ge(acc_done, s)
                nc.vector.tensor_tensor(cnt[:, ds(base, WIN)], ps_cnt, cnt[:, ds(base, WIN)], ALU.add)
                nc.vector.tensor_tensor(acc[:, ds(base, WIN)], ps_sum, acc[:, ds(base, WIN)], ALU.add
                                        ).then_inc(acc_done, 1)

            for s in range(SLOTS):
                make_hot(s, s, True)
                if s >= 2:
                    add_z(s - 2, s - 2, 1)
                if s >= 3:
                    accumulate(s - 3, s - 3, s == 3)
            with dve.Fori(1, bodies) as it:
                for u in range(SLOTS):
                    s = it * SLOTS + u
                    make_hot(s, u, False)
                    add_z(s - 2, (u - 2) % SLOTS, it + 1 if u >= 2 else it)
                    accumulate(s - 3, (u - 3) % SLOTS, False)
            add_z(groups - 2, SLOTS - 2, bodies)
            accumulate(groups - 3, SLOTS - 3, False)
            add_z(groups - 1, SLOTS - 1, bodies)
            accumulate(groups - 2, SLOTS - 2, False)
            accumulate(groups - 1, SLOTS - 1, False)

            dve.wait_ge(cov_summed, 1)
            nc.vector.tensor_scalar(flag[:], ps_sum[0:1, 0:1], -1.0, float(n_edges), ALU.mult, ALU.add
                                    ).then_inc(flag_ready, 1)
            dve.wait_ge(flag_ready, 1)
            outside = dve.value_load(flag[0:1, 0:1], min_val=0, max_val=n_edges)
            with dve.If(outside > 0):
                with dve.Fori(0, n_tiles) as t:
                    dve.wait_ge(g_idx_in, 32 * (t + 1))
                    nc.vector.tensor_scalar(gen_dst[:, 0:1], inside[:, ds(t, 1)], -1.0, 1.0, ALU.mult, ALU.add
                                            ).then_inc(g_step, 1)
                    dve.wait_ge(g_step, 4 * t + 1)
                    nc.vector.scalar_tensor_tensor(gen_dst[:, 1:2], gen_idx[:, 1:2], 1.0, gen_dst[:, 0:1],
                                                   ALU.add, ALU.mult).then_inc(g_step, 1)
                    dve.wait_ge(g_step, 4 * t + 2)
                    nc.vector.scalar_tensor_tensor(gen_rel[:], gen_dst[:, 1:2].to_broadcast([P, gen_k]), -1.0,
                                                   gen_off[:], ALU.add, ALU.subtract)
                    dve.wait_ge(g_gathered, 32 * (t + 1))
                    dve.wait_ge(g_z, t + 1)
                    nc.vector.tensor_tensor(gen_z, ps[:, 0, 0:hidden], gen_b, ALU.add).then_inc(g_step, 1)
                    dve.wait_ge(g_step, 4 * t + 3)
                    nc.vector.tensor_tensor(gen_z, gen_z, gen_a, ALU.add).then_inc(g_step, 1)
                    dve.wait_ge(g_step, 4 * t + 4)
                    dve.sem_inc(waited)
                    with dve.Fori(0, rounds) as r:
                        k = t * rounds + r
                        nc.vector.tensor_tensor(gen_oh3, iota_gen[:].unsqueeze(1).to_broadcast([P, gen_k, gen_cols]),
                                                gen_rel[:].unsqueeze(2).to_broadcast([P, gen_k, gen_cols]),
                                                ALU.is_equal).then_inc(g_hot, 1)
                        dve.wait_ge(g_hot, k + 1)
                        nc.vector.tensor_scalar(gen_rel[:], gen_rel[:], float(gen_k * gen_cols), None, ALU.subtract)
                        dve.wait_ge(g_sum, k + 1)
                        for rows, part in ((cnt[:], ps[0:1, 0:gen_k, gen_cols:2 * gen_cols]),
                                           (acc[:], ps[:, 0:gen_k, 0:gen_cols])):
                            nodes = rows[:, ds(r * (gen_k * gen_cols), gen_k * gen_cols)].rearrange(
                                "p (k n) -> p k n", k=gen_k)
                            last = nc.vector.tensor_tensor(nodes, part, nodes, ALU.add)
                        last.then_inc(g_acc, 1)
                        dve.wait_ge(g_acc, k + 1)
            with dve.Else():
                dve.nop()
            nc.vector.memset(gen_dst[:, 0:1], 0.0).then_inc(sums_complete, 1)

            def finish(n, u, fills):
                dve.wait_ge(fin_prod, n + 1)
                dve.wait_ge(fin_in[u], 16 * (fills + 1))
                if not isinstance(fills, int) or fills > 0:
                    dve.wait_ge(fin_stored[u], 16 * fills)
                nc.vector.tensor_tensor(fin_o[:, u, 0:fin_cols], ps[0:feat, u, 0:fin_cols], fin_x[:, u, 0:fin_cols],
                                        ALU.add).then_inc(fin_ready, 1)

            for u in range(SLOTS):
                finish(u, u, 0)
            with dve.Fori(1, fin_steps // SLOTS) as it:
                for u in range(SLOTS):
                    finish(it * SLOTS + u, u, it)

        @block.tensor
        def _(pe):
            def turn_h(c, u, first):
                pe.wait_ge(h_ready, c + 1)
                if not first:
                    pe.wait_ge(ht_ready, c * units + u - (1 if u == 0 else 2) + 1)
                pe.sem_inc(waited)
                for j in range(2):
                    last = nc.tensor.transpose(ps_ht[:, u % 2, j * P:(j + 1) * P], h_sb[:, 2 * u + j, :], ident[:])
                last.then_inc(h_turned, 1)

            def products(c, u, first):
                pe.wait_ge(ht_ready, c * units + u + 1)
                for n, (bank, taken) in enumerate(((ps_b, b_ready), (ps_a, a_ready))):
                    if not first or u >= 3:
                        pe.wait_ge(taken, c * units + u - prod_gap[u] + 1)
                    for j in range(2):
                        last = nc.tensor.matmul(bank[:, prod_slot[u], j, :], h_t[:, u, j * P:(j + 1) * P],
                                                w_ba[:, n * hidden:(n + 1) * hidden], start=True, stop=True)
                last.then_inc(prod_ready, 1)

            pe.wait_ge(ident_ready, 1)
            for u in range(units):
                turn_h(0, u, u < 2)
            pe.wait_ge(w_in, 32)

            def chunk(c, first, more):
                for u in range(units):
                    products(c, u, first)
                    if more:
                        turn_h(c + 1, u, False)

            chunk(0, True, True)
            with pe.Fori(1, chunks - 1) as c:
                chunk(c, False, True)
            pe.wait_ge(ones_ready, 2)
            pe.wait_ge(base_ready, 1)
            pe.wait_ge(ht_ready, chunks * units)
            half = (groups + 1) // 2
            for k in range(2):
                g0, g1 = k * half, min(groups, (k + 1) * half)
                last = nc.tensor.matmul(ps_base[:, k, 0:g1 - g0], ones_row[:], base_f[:, g0:g1], start=True, stop=True)
            last.then_inc(base_spread, 1)
            chunk(chunks - 1, False, False)

            pe.wait_ge(we_in, 16 * SLOTS)
            pe.wait_ge(b_ready, chunks * units)
            pe.wait_ge(a_ready, chunks * units)
            pe.wait_ge(rel_ready, 2)

            def turn_hot(s, u, first):
                pe.wait_ge(hot_ready, s + 1)
                if not first:
                    pe.wait_ge(lhs_ready, s)
                pe.sem_inc(waited)
                for t in range(TILES):
                    last = nc.tensor.transpose(ps_oht[:, t * P:(t + 1) * P], onehot[:, u, t, :], ident[:])
                last.then_inc(hot_turned, 1)

            def gap(u):
                return (1, 3, 2, 2, 2)[u]

            def make_z(s, u, first, fills):
                pe.wait_ge(lhs_ready, s + 1)
                pe.wait_ge(loaded[u], 32 * fills)
                if not first:
                    pe.wait_ge(z_added, s - gap(u) + 1)
                for t in range(TILES):
                    last = nc.tensor.matmul(ps_z[:, u % 2, t * P:(t + 1) * P], lhs[:, u, t * P:(t + 1) * P],
                                            rhs[:, u, :], start=True, stop=True)
                last.then_inc(z_ready, 1)

            def make_sums(s, u, first):
                pe.wait_ge(r_ready, s + 1)
                if not first:
                    pe.wait_ge(acc_done, s)
                for t in range(TILES):
                    nc.tensor.matmul(ps_sum, gath[:, u, t, :], onehot[:, u, t, :],
                                     start=(t == 0), stop=(t == TILES - 1))
                for t in range(TILES):
                    last = nc.tensor.matmul(ps_cnt, ones_col[:], onehot[:, u, t, :],
                                            start=(t == 0), stop=(t == TILES - 1))
                last.then_inc(summed, 1)

            for s in range(SLOTS):
                if s >= 3:
                    make_sums(s - 3, s - 3, s == 3)
                turn_hot(s, s, s == 0)
                if s >= 1:
                    make_z(s - 1, s - 1, s - 1 < 2, 1)
            with pe.Fori(1, bodies) as it:
                for u in range(SLOTS):
                    s = it * SLOTS + u
                    make_sums(s - 3, (u - 3) % SLOTS, False)
                    turn_hot(s, u, False)
                    make_z(s - 1, (u - 1) % SLOTS, False, it + 1 if u >= 1 else it)
            make_sums(groups - 3, SLOTS - 3, False)
            make_z(groups - 1, SLOTS - 1, False, bodies)
            make_sums(groups - 2, SLOTS - 2, False)
            make_sums(groups - 1, SLOTS - 1, False)

            pe.wait_ge(inside_step, 2)
            pe.wait_ge(acc_done, groups)
            nc.tensor.matmul(ps_sum[0:1, 0:1], covered[:], ones_col[:], start=True, stop=True).then_inc(cov_summed, 1)

            pe.wait_ge(flag_ready, 1)
            outside = pe.value_load(flag[0:1, 0:1], min_val=0, max_val=n_edges)
            with pe.If(outside > 0):
                with pe.Fori(0, n_tiles) as t:
                    pe.wait_ge(g_e_in, 16 * (t + 1))
                    nc.tensor.matmul(ps[:, 0, 0:hidden], lhs[e_row:k_rows, 1, 0:P], rhs[e_row:k_rows, 0, :],
                                     start=True, stop=True).then_inc(g_z, 1)
                    pe.wait_ge(g_r, t + 1)
                    pe.sem_inc(waited)
                    with pe.Fori(0, rounds) as r:
                        pe.wait_ge(g_hot, t * rounds + r + 1)
                        for k in range(gen_k):
                            nc.tensor.matmul(ps[:, k, 0:gen_cols], gen_z, gen_oh3[:, k, :], start=True, stop=True)
                            last = nc.tensor.matmul(ps[0:1, k, gen_cols:2 * gen_cols], ones_col[:], gen_oh3[:, k, :],
                                                    start=True, stop=True)
                        last.then_inc(g_sum, 1)
            with pe.Else():
                pe.nop()

            pe.wait_ge(sums_complete, 1)
            pe.wait_ge(last_w_in, 32)

            def last_products(n, u, first):
                if not first:
                    pe.wait_ge(fin_ready, n - SLOTS + 1)
                nc.tensor.matmul(ps[:, u, 0:fin_cols], w2_sb[:], acc[:, ds(n * fin_cols, fin_cols)],
                                 start=True, stop=False)
                nc.tensor.matmul(ps[:, u, 0:fin_cols], b2_sb[:], cnt[:, ds(n * fin_cols, fin_cols)],
                                 start=False, stop=True).then_inc(fin_prod, 1)

            for u in range(SLOTS):
                last_products(u, u, True)
            with pe.Fori(1, fin_steps // SLOTS) as it:
                for u in range(SLOTS):
                    last_products(it * SLOTS + u, u, False)


_INS = ["x", "x_t", "src_t", "dst_t", "edge_t", "w1", "b1", "w2", "b2"]


def kernel(x, src, dst, edge_attr_32, L0_gnn_W1, L0_gnn_b1, L0_gnn_W2, L0_gnn_b2):
    import numpy as np
    from concourse import bacc
    from concourse.bass_utils import run_bass_kernel_spmd

    x = np.asarray(x)
    given = [
        x, x.T, np.asarray(src).reshape(-1, P).T, np.asarray(dst).reshape(-1, P).T, np.asarray(edge_attr_32).T,
        np.asarray(L0_gnn_W1), np.asarray(L0_gnn_b1), np.asarray(L0_gnn_W2), np.asarray(L0_gnn_b2).reshape(1, -1),
    ]
    nc = bacc.Bacc("TRN2", target_bir_lowering=False, num_devices=1)
    arrays, args = {}, []
    for name, a in zip(_INS, given):
        a = np.ascontiguousarray(a)
        arrays[f"in_{name}"] = a
        args.append(nc.dram_tensor(f"in_{name}", a.shape, mybir.dt.from_np(a.dtype), kind="ExternalInput").ap())
    out = nc.dram_tensor("out_t", (x.shape[1], x.shape[0]), F32, kind="ExternalOutput").ap()
    gnn(nc, *args, out)
    r = run_bass_kernel_spmd(nc, [arrays], core_ids=[0])
    return np.ascontiguousarray(r.results[0]["out_t"].T)
```

```python
from contextlib import ExitStack

import concourse.bass as bass
from concourse import mybir

F32 = mybir.dt.float32
I32 = mybir.dt.int32
ALU = mybir.AluOpType
ACT = mybir.ActivationFunctionType
AX = mybir.AxisListType
ds = bass.ds

P = 128
BANK = 512
TILES = 5
SLOTS = 5
WIN = 64
EPS = 1e-5


def gnn(nc, x_main, x_last, x_t, src_t, dst_t, edge_t, w1, b1, w2, b2, out_t):
    feat, n_nodes = x_t.shape
    edge_feat, n_edges = edge_t.shape
    hidden = w1.shape[1]
    n_tiles = n_edges // P
    groups = n_tiles // TILES
    bodies = groups // SLOTS
    full = n_nodes // P
    last = n_nodes - full * P
    node_tiles = full + 1
    padded = node_tiles * P
    chunk_tiles, units = 14, 7
    chunks = node_tiles // chunk_tiles
    e_cols = TILES * P
    e_row = WIN
    one_row = e_row + edge_feat
    k_rows = one_row + 1
    h_row = 64
    h_end = h_row + feat
    gen_cols, gen_k = 500, 5
    rounds = n_nodes // (gen_cols * gen_k)
    assert hidden == P and 0 < last < P and feat <= h_row and h_end <= P
    assert chunks * chunk_tiles == node_tiles and chunk_tiles == 2 * units
    assert n_tiles * P == n_edges and bodies * SLOTS * TILES == n_tiles and bodies >= 2
    assert rounds * gen_cols * gen_k == n_nodes

    a_table = nc.dram_tensor("a_table", [padded, hidden], F32).ap()
    b_table = nc.dram_tensor("b_table", [padded, hidden], F32).ap()

    ctx = ExitStack()
    with ctx:
        def sb(name, shape, dt=F32):
            return ctx.enter_context(nc.sbuf_tensor(name, shape, dt))

        def sem(name):
            return ctx.enter_context(nc.semaphore(name))

        nodes = sb("nodes", [h_end, padded])
        src_sb = sb("src_sb", [P, n_tiles], I32)
        dst_sb = sb("dst_sb", [P, n_tiles], I32)
        dst_rel = sb("dst_rel", [P, n_tiles])
        gath = sb("gath", [P, SLOTS, TILES, hidden])
        lhs = sb("lhs", [k_rows, SLOTS, e_cols])
        rhs = sb("rhs", [k_rows, SLOTS, hidden])
        onehot = sb("onehot", [P, SLOTS, TILES, WIN])
        h_win = sb("h_win", [h_end, SLOTS, WIN])
        sums = sb("sums", [P, WIN])
        idx = sb("idx", [P, SLOTS, TILES], I32)
        x_sb = sb("x_sb", [P, node_tiles, feat])
        h_sb = sb("h_sb", [P, chunk_tiles, feat])
        sq_sb = sb("sq_sb", [P, chunk_tiles, feat])
        stat = sb("stat", [P, 5, chunk_tiles])
        h_t = sb("h_t", [h_end, units, 2 * P])
        b_stage = sb("b_stage", [P, units, 2, hidden])
        w_b = sb("w_b", [h_end, hidden])
        w_a = sb("w_a", [h_end, hidden])
        w2_sb = sb("w2_sb", [hidden, feat])
        b2_bc = sb("b2_bc", [P, feat])
        ident = sb("ident", [P, P])
        ones_row = sb("ones_row", [1, P])
        ones_col = sb("ones_col", [P, 1])
        iota_gen = sb("iota_gen", [P, gen_cols])
        base_f = sb("base_f", [1, groups])
        base_i = sb("base_i", [1, groups], I32)
        covered = sb("covered", [P, 1])
        flag = sb("flag", [1, 1], I32)
        gen_idx = sb("gen_idx", [P, 2], I32)
        gen_dst = sb("gen_dst", [P, 2])
        gen_rel = sb("gen_rel", [P, gen_k])
        gen_off = sb("gen_off", [P, gen_k])
        gen_oh = sb("gen_oh", [P, gen_k, gen_cols])
        gen_msg = sb("gen_msg", [P, feat])

        out_sb = nodes[0:feat, 0:n_nodes]
        h_all = nodes[h_row:h_end, :]
        inside = dst_sb[:].bitcast(F32)
        gen_z = gath[:, 0, 0, :]
        gen_b = gath[:, 1, 0, :]
        gen_a = gath[:, 2, 0, :]
        gen_zt = gath[:, 3, 0, :]

        ps = ctx.enter_context(nc.psum_tensor("ps", [P, 8, BANK], F32))
        ps_b = ps[:, 0:3, 0:2 * hidden].rearrange("p s (j w) -> p s j w", j=2)
        ps_ht = ps[0:feat, 4:6, 0:2 * P]
        ps_base = ps[:, 6:8, :]
        ps_z = ps[:, 0:4, :].rearrange("p (s b) c -> p s (b c)", b=2)[:, :, 0:e_cols]
        ps_win = ps[0:WIN, 4:6, :].rearrange("p b c -> p (b c)")
        ps_oht = ps_win[:, 0:e_cols]
        ps_aw = ps_win[:, 2 * BANK - hidden:2 * BANK]
        ps_sum = ps[:, 6, 0:WIN]
        ps_out = ps[0:feat, 6, WIN:2 * WIN]
        iota_ps = ps[:, 7, 0:WIN]

        x_first, x_rest, x_tail, xt_in = sem("x_first"), sem("x_rest"), sem("x_tail"), sem("xt_in")
        w_in, we_in, w2_in = sem("w_in"), sem("we_in"), sem("w2_in")
        dst_in, src_in = sem("dst_in"), sem("src_in")
        tail_zero, ident_zero, ident_ready = sem("tail_zero"), sem("ident_zero"), sem("ident_ready")
        ones_ready, iota_ready, iota_copied = sem("ones_ready"), sem("iota_ready"), sem("iota_copied")
        base_ready, base_spread, rel_ready, inside_step = sem("base_ready"), sem("base_spread"), sem("rel_ready"), sem("inside_step")
        cov_summed, flag_ready = sem("cov_summed"), sem("flag_ready")
        stat_step, var_ready, std_ready, rstd_ready = sem("stat_step"), sem("var_ready"), sem("std_ready"), sem("rstd_ready")
        h_ready, h_turned, ht_ready, ht_kept = sem("h_ready"), sem("h_turned"), sem("ht_ready"), sem("ht_kept")
        prod_ready, b_ready = sem("prod_ready"), sem("b_ready")
        b_stored = [sem(f"b_stored{u}") for u in range(units)]
        idx_ready, hot_ready, hot_turned, lhs_ready = sem("idx_ready"), sem("hot_ready"), sem("hot_turned"), sem("lhs_ready")
        gathered = [sem(f"gathered{u}") for u in range(SLOTS)]
        loaded = [sem(f"loaded{u}") for u in range(SLOTS)]
        win_loaded = [sem(f"win_loaded{u}") for u in range(SLOTS)]
        z_ready, z_added, r_ready = sem("z_ready"), sem("z_added"), sem("r_ready")
        summed, sums_copied, folded, out_added = sem("summed"), sem("sums_copied"), sem("folded"), sem("out_added")
        sums_complete, out_stored = sem("sums_complete"), sem("out_stored")
        t_h, t_prod, t_out, t_stored = sem("t_h"), sem("t_prod"), sem("t_out"), sem("t_stored")
        g_idx_in, g_e_in, g_gathered = sem("g_idx_in"), sem("g_e_in"), sem("g_gathered")
        g_z, g_step, g_r, g_turned, g_rt = sem("g_z"), sem("g_step"), sem("g_r"), sem("g_turned"), sem("g_rt")
        g_prod, g_msg, g_hot, g_sum, g_acc = sem("g_prod"), sem("g_msg"), sem("g_hot"), sem("g_sum"), sem("g_acc")

        b_rows = b_table.rearrange("(j p) h -> p j h", p=P)

        prod_slot = (0, 1, 2, 0, 1, 2, 1)
        prod_gap = (4, 2, 4, 3, 3, 3, 2)

        waited = sem("waited")

        block = ctx.enter_context(nc.Block())

        @block.sync
        def _(sp):
            sp.dma_start(x_sb[:, 0:chunk_tiles, :], x_main[:, 0:chunk_tiles, :]).then_inc(x_first, 16)
            sp.dma_start(w_b[h_row:h_end, :], w1[feat:2 * feat, :]).then_inc(w_in, 16)
            sp.dma_start(x_sb[:, chunk_tiles:full, :], x_main[:, chunk_tiles:full, :]).then_inc(x_rest, 16)
            sp.wait_ge(tail_zero, 1)
            sp.dma_start(x_sb[0:last, full, :], x_last).then_inc(x_tail, 16)
            sp.dma_start(dst_sb[:], dst_t).then_inc(dst_in, 16)
            sp.dma_start(src_sb[:], src_t).then_inc(src_in, 16)
            sp.dma_start(w_a[h_row:h_end, :], w1[0:feat, :]).then_inc(w_in, 16)
            for s in range(SLOTS):
                sp.dma_start(rhs[e_row:one_row, s, :], w1[2 * feat:2 * feat + edge_feat, :]).then_inc(we_in, 16)
                sp.dma_start(rhs[one_row:k_rows, s, :], b1).then_inc(we_in, 16)
            sp.dma_start(w2_sb[:], w2).then_inc(w2_in, 16)
            sp.dma_start(b2_bc[:], b2.partition_broadcast(P)).then_inc(w2_in, 16)
            sp.dma_start(out_sb, x_t).then_inc(xt_in, 16)

            with sp.Fori(0, chunks) as c:
                for u in range(units):
                    sp.wait_ge(b_ready, c * units + u + 1)
                    sp.dma_start(b_rows[:, ds(c * chunk_tiles + 2 * u, 2), :], b_stage[:, u, :, :]).then_inc(b_stored[u], 16)

            sp.wait_ge(base_ready, 2)
            sp.wait_ge(ht_kept, chunks * units)

            def load_group(s, u, first):
                if not first:
                    sp.wait_ge(z_ready, s - SLOTS + 1)
                sp.dma_start(lhs[e_row:one_row, u, :], edge_t[:, ds(s * e_cols, e_cols)]).then_inc(loaded[u], 16)
                base = sp.value_load(base_i[0:1, ds(s, 1)], min_val=0, max_val=n_nodes - WIN)
                sp.dma_start(h_win[h_row:h_end, u, :], h_all[:, ds(base, WIN)]).then_inc(win_loaded[u], 16)

            for u in range(SLOTS):
                load_group(u, u, True)
            with sp.Fori(1, bodies) as it:
                for u in range(SLOTS):
                    load_group(it * SLOTS + u, u, False)

            sp.wait_ge(flag_ready, 1)
            outside = sp.value_load(flag[0:1, 0:1], min_val=0, max_val=n_edges)
            with sp.If(outside > 0):
                with sp.Fori(0, node_tiles) as j:
                    sp.wait_ge(t_out, j + 1)
                    sp.dma_start(a_table[ds(j * P, P), :], gen_a).then_inc(t_stored, 16)

                def load_tile(t):
                    sp.dma_start(gen_idx[:, 0:1], src_t[:, ds(t, 1)], allow_slow_non_contiguous=True).then_inc(g_idx_in, 16)
                    sp.dma_start(gen_idx[:, 1:2], dst_t[:, ds(t, 1)], allow_slow_non_contiguous=True).then_inc(g_idx_in, 16)
                    sp.dma_start(lhs[e_row:one_row, 1, 0:P], edge_t[:, ds(t * P, P)]).then_inc(g_e_in, 16)

                load_tile(0)
                with sp.Fori(1, n_tiles) as t:
                    sp.wait_ge(g_acc, t * rounds)
                    sp.sem_inc(waited)
                    load_tile(t)
            with sp.Else():
                sp.nop()

            sp.wait_ge(sums_complete, 1)
            sp.dma_start(out_t, out_sb).then_inc(out_stored, 16)
            sp.wait_ge(out_stored, 16)

        @block.gpsimd
        def _(pool):
            nc.gpsimd.memset(x_sb[:, full, :], 0.0).then_inc(tail_zero, 1)
            nc.gpsimd.memset(ident[:], 0.0).then_inc(ident_zero, 1)
            pool.wait_ge(ident_zero, 1)
            nc.gpsimd.affine_select(out=ident[:], in_=ident[:], compare_op=ALU.not_equal, fill=1.0, base=0,
                                    pattern=[[-1, P]], channel_multiplier=1).then_inc(ident_ready, 1)
            nc.gpsimd.memset(ones_row[:], 1.0).then_inc(ones_ready, 1)
            nc.gpsimd.memset(ones_col[:], 1.0).then_inc(ones_ready, 1)
            pool.wait_ge(ones_ready, 2)
            nc.gpsimd.memset(lhs[one_row:k_rows, :, :], 1.0).then_inc(ones_ready, 1)
            pool.wait_ge(ones_ready, 3)
            nc.gpsimd.iota(iota_gen[:], [[1, gen_cols]], base=0, channel_multiplier=0,
                           allow_small_or_imprecise_dtypes=True).then_inc(iota_ready, 1)
            nc.gpsimd.iota(gen_off[:], [[gen_cols, gen_k]], base=0, channel_multiplier=0,
                           allow_small_or_imprecise_dtypes=True).then_inc(iota_ready, 1)

            pool.wait_ge(iota_ready, 2)
            with pool.Fori(0, chunks) as c:
                for u in range(units):
                    pool.wait_ge(ht_ready, c * units + u + 1)
                    nc.gpsimd.tensor_copy(h_all[:, ds(c * (chunk_tiles * P) + u * 2 * P, 2 * P)],
                                          h_t[h_row:h_end, u, :]).then_inc(ht_kept, 1)

            pool.wait_ge(ht_kept, chunks * units)
            for u in range(units):
                pool.wait_ge(b_stored[u], 16 * chunks)

            def gather_group(s, u):
                pool.wait_ge(idx_ready, s + 1)
                pool.sem_inc(waited)
                for t in range(TILES):
                    pool.indirect_dma_start(
                        gath[:, u, t, :], None, b_table,
                        bass.IndirectOffsetOnAxis(ap=idx[:, u, t:t + 1], axis=0)).then_inc(gathered[u], 16)

            for u in range(SLOTS):
                gather_group(u, u)
            with pool.Fori(1, bodies) as it:
                for u in range(SLOTS):
                    gather_group(it * SLOTS + u, u)

            outside = pool.value_load(flag[0:1, 0:1], min_val=0, max_val=n_edges)
            with pool.If(outside > 0):
                pool.wait_ge(t_stored, 16 * node_tiles)
                with pool.Fori(0, n_tiles) as t:
                    pool.wait_ge(g_idx_in, 32 * (t + 1))
                    pool.sem_inc(waited)
                    pool.indirect_dma_start(gen_b, None, b_table, bass.IndirectOffsetOnAxis(
                        ap=gen_idx[:, 0:1], axis=0)).then_inc(g_gathered, 16)
                    pool.indirect_dma_start(gen_a, None, a_table, bass.IndirectOffsetOnAxis(
                        ap=gen_idx[:, 1:2], axis=0)).then_inc(g_gathered, 16)
            with pool.Else():
                pool.nop()

        @block.scalar
        def _(act):
            def root(c):
                act.wait_ge(var_ready, c + 1)
                nc.scalar.activation(stat[:, 3, :], stat[:, 2, :], ACT.Sqrt).then_inc(std_ready, 1)

            def take_ht(c, u, first):
                act.wait_ge(h_turned, c * units + u + 1)
                if not first:
                    act.wait_ge(ht_kept, (c - 1) * units + u + 1)
                nc.scalar.copy(h_t[h_row:h_end, u, :], ps_ht[:, u % 2, :]).then_inc(ht_ready, 1)

            def take_b(c, u, first):
                act.wait_ge(prod_ready, c * units + u + 1)
                if not first:
                    act.wait_ge(b_stored[u], 16 * c)
                nc.scalar.copy(b_stage[:, u, :, :], ps_b[:, prod_slot[u], :, :]).then_inc(b_ready, 1)

            root(0)
            for u in range(units):
                take_ht(0, u, True)
            root(1)

            def chunk(c, first, ht, stats):
                for u in range(units):
                    take_b(c, u, first)
                    if ht:
                        take_ht(c + 1, u, False)
                    if stats and u == 3:
                        root(c + 2)

            chunk(0, True, True, True)
            with act.Fori(1, chunks - 2) as c:
                chunk(c, False, True, True)
            chunk(chunks - 2, False, True, False)
            act.wait_ge(src_in, 16)

            def take_idx(s, u, first):
                if not first:
                    act.wait_ge(summed, s - SLOTS + 1)
                nc.scalar.copy(idx[:, u, :], src_sb[:, ds(s * TILES, TILES)]).then_inc(idx_ready, 1)

            take_idx(0, 0, True)
            take_idx(1, 1, True)
            chunk(chunks - 1, False, False, False)
            act.wait_ge(iota_ready, 2)
            act.wait_ge(rel_ready, 2)
            nc.scalar.copy(iota_ps, iota_gen[:, 0:WIN]).then_inc(iota_copied, 1)

            def take_hot(s, u, first):
                act.wait_ge(hot_turned, s + 1)
                if not first:
                    act.wait_ge(z_ready, s - SLOTS + 1)
                nc.scalar.copy(rhs[0:WIN, u, :], ps_aw)
                nc.scalar.copy(lhs[0:WIN, u, :], ps_oht).then_inc(lhs_ready, 1)

            def rectify(s, u):
                act.wait_ge(z_added, s + 1)
                z = gath[:, u, :, :]
                nc.scalar.activation(z, z, ACT.Relu).then_inc(r_ready, 1)

            for s in range(SLOTS):
                if s >= 2:
                    take_idx(s, s, True)
                take_hot(s, s, True)
                if s >= 2:
                    rectify(s - 2, s - 2)
            with act.Fori(1, bodies) as it:
                for u in range(SLOTS):
                    s = it * SLOTS + u
                    take_idx(s, u, False)
                    take_hot(s, u, False)
                    rectify(s - 2, (u - 2) % SLOTS)
            rectify(groups - 2, SLOTS - 2)
            rectify(groups - 1, SLOTS - 1)

            outside = act.value_load(flag[0:1, 0:1], min_val=0, max_val=n_edges)
            with act.If(outside > 0):
                def take_tile(j):
                    nc.scalar.copy(h_t[h_row:h_end, 0, 0:P], h_all[:, ds(j * P, P)]).then_inc(t_h, 1)

                take_tile(0)
                with act.Fori(1, node_tiles) as j:
                    act.wait_ge(t_stored, 16 * j)
                    take_tile(j)
                with act.Fori(0, n_tiles) as t:
                    act.wait_ge(g_step, 4 * t + 4)
                    nc.scalar.activation(gen_z, gen_z, ACT.Relu).then_inc(g_r, 1)
                    act.wait_ge(g_turned, t + 1)
                    nc.scalar.copy(gen_zt, ps[:, 1, 0:P]).then_inc(g_rt, 1)
            with act.Else():
                act.nop()

        @block.vector
        def _(dve):
            def stats(c, chained):
                xc = x_sb[:, ds(c * chunk_tiles, chunk_tiles), :]
                nc.vector.tensor_reduce(stat[:, 0, :], xc, AX.X, ALU.add).then_inc(stat_step, 1)
                dve.wait_ge(stat_step, 4 * c + 1)
                nc.vector.scalar_tensor_tensor(
                    xc, stat[:, 0, :].unsqueeze(2).to_broadcast([P, chunk_tiles, feat]), -1.0 / feat, xc,
                    ALU.mult, ALU.add).then_inc(stat_step, 1)
                dve.wait_ge(stat_step, 4 * c + 2)
                nc.vector.tensor_tensor(sq_sb[:], xc, xc, ALU.mult).then_inc(stat_step, 1)
                dve.wait_ge(stat_step, 4 * c + 3)
                nc.vector.tensor_reduce(stat[:, 1, :], sq_sb[:], AX.X, ALU.add).then_inc(stat_step, 1)
                dve.wait_ge(stat_step, 4 * c + 4)
                nc.vector.tensor_scalar(stat[:, 2, :], stat[:, 1, :], 1.0 / feat, EPS, ALU.mult, ALU.add
                                        ).then_inc(var_ready, 1)
                dve.wait_ge(std_ready, c + 1)
                if chained:
                    dve.wait_ge(h_ready, c)
                nc.vector.reciprocal(stat[:, 4, :], stat[:, 3, :]).then_inc(rstd_ready, 1)

            def write_h(c, first):
                dve.wait_ge(rstd_ready, c + 1)
                if not first:
                    dve.wait_ge(h_turned, c * units)
                nc.vector.scalar_tensor_tensor(
                    h_sb[:], x_sb[:, ds(c * chunk_tiles, chunk_tiles), :], 0.0,
                    stat[:, 4, :].unsqueeze(2).to_broadcast([P, chunk_tiles, feat]),
                    ALU.max, ALU.mult).then_inc(h_ready, 1)

            dve.wait_ge(x_first, 16)
            stats(0, False)
            write_h(0, True)
            dve.wait_ge(x_rest, 16)
            dve.wait_ge(x_tail, 16)
            with dve.Fori(1, chunks) as c:
                stats(c, True)
                write_h(c, False)

            dve.wait_ge(dst_in, 16)
            firsts = dst_sb[0:1, :].rearrange("p (g t) -> p g t", t=TILES)[:, :, 0]
            nc.vector.tensor_scalar(base_f[:], firsts, float(n_nodes - WIN), None, ALU.min).then_inc(base_ready, 1)
            nc.vector.tensor_scalar(base_i[:], firsts, float(n_nodes - WIN), None, ALU.min).then_inc(base_ready, 1)
            dve.wait_ge(base_spread, 1)
            half = (groups + 1) // 2
            for k in range(2):
                g0, g1 = k * half, min(groups, (k + 1) * half)
                nc.vector.tensor_tensor(
                    dst_rel[:, g0 * TILES:g1 * TILES].rearrange("p (g t) -> p g t", t=TILES),
                    dst_sb[:, g0 * TILES:g1 * TILES].rearrange("p (g t) -> p g t", t=TILES),
                    ps_base[:, k, 0:g1 - g0].unsqueeze(2).to_broadcast([P, g1 - g0, TILES]),
                    ALU.subtract).then_inc(rel_ready, 1)
            dve.wait_ge(rel_ready, 2)
            nc.vector.tensor_scalar(inside, dst_rel[:], 0.0, None, ALU.is_ge).then_inc(inside_step, 1)
            dve.wait_ge(inside_step, 1)
            nc.vector.scalar_tensor_tensor(inside, dst_rel[:], float(WIN), inside, ALU.is_lt, ALU.mult,
                                           accum_out=covered[:]).then_inc(inside_step, 1)
            dve.wait_ge(cov_summed, 1)
            nc.vector.tensor_scalar(flag[:], ps_sum[0:1, 0:1], -1.0, float(n_edges), ALU.mult, ALU.add
                                    ).then_inc(flag_ready, 1)
            dve.wait_ge(iota_copied, 1)
            dve.wait_ge(xt_in, 16)

            def make_hot(s, u, first):
                if not first:
                    dve.wait_ge(folded, s - SLOTS + 1)
                nc.vector.tensor_tensor(
                    onehot[:, u, :, :], iota_ps.unsqueeze(1).to_broadcast([P, TILES, WIN]),
                    dst_rel[:, ds(s * TILES, TILES)].unsqueeze(2).to_broadcast([P, TILES, WIN]),
                    ALU.is_equal).then_inc(hot_ready, 1)

            def add_z(s, u, fills):
                dve.wait_ge(z_ready, s + 1)
                dve.wait_ge(gathered[u], 16 * TILES * fills)
                z = gath[:, u, :, :].rearrange("p t h -> p (t h)")
                nc.vector.tensor_tensor(z, ps_z[:, u % 2, :], z, ALU.add).then_inc(z_added, 1)

            def copy_sums(s):
                dve.wait_ge(summed, s + 1)
                nc.vector.tensor_copy(sums[:], ps_sum).then_inc(sums_copied, 1)

            def add_out(s, first, alone=False):
                dve.wait_ge(folded, s + 1)
                if not alone:
                    dve.wait_ge(summed, s + 2)
                if not first:
                    dve.wait_ge(out_added, s)
                base = dve.value_load(base_i[0:1, ds(s, 1)], min_val=0, max_val=n_nodes - WIN)
                nc.vector.tensor_tensor(out_sb[:, ds(base, WIN)], ps_out, out_sb[:, ds(base, WIN)], ALU.add
                                        ).then_inc(out_added, 1)

            for s in range(SLOTS):
                make_hot(s, s, True)
                if s >= 2:
                    add_z(s - 2, s - 2, 1)
                if s >= 4:
                    add_out(s - 4, True)
                if s >= 3:
                    copy_sums(s - 3)
            with dve.Fori(1, bodies) as it:
                for u in range(SLOTS):
                    s = it * SLOTS + u
                    make_hot(s, u, False)
                    add_z(s - 2, (u - 2) % SLOTS, it + 1 if u >= 2 else it)
                    add_out(s - 4, False)
                    copy_sums(s - 3)
            add_z(groups - 2, SLOTS - 2, bodies)
            add_out(groups - 4, False)
            copy_sums(groups - 3)
            add_z(groups - 1, SLOTS - 1, bodies)
            for s in range(groups - 3, groups - 1):
                add_out(s, False)
                copy_sums(s + 1)
            add_out(groups - 1, False, alone=True)

            outside = dve.value_load(flag[0:1, 0:1], min_val=0, max_val=n_edges)
            with dve.If(outside > 0):
                with dve.Fori(0, node_tiles) as j:
                    dve.wait_ge(t_prod, j + 1)
                    nc.vector.tensor_copy(gen_a, ps[:, 0, 0:hidden]).then_inc(t_out, 1)
                with dve.Fori(0, n_tiles) as t:
                    dve.wait_ge(g_idx_in, 32 * (t + 1))
                    nc.vector.tensor_scalar(gen_dst[:, 0:1], inside[:, ds(t, 1)], -1.0, 1.0, ALU.mult, ALU.add
                                            ).then_inc(g_step, 1)
                    dve.wait_ge(g_step, 4 * t + 1)
                    nc.vector.scalar_tensor_tensor(gen_dst[:, 1:2], gen_idx[:, 1:2], 1.0, gen_dst[:, 0:1],
                                                   ALU.add, ALU.mult).then_inc(g_step, 1)
                    dve.wait_ge(g_step, 4 * t + 2)
                    nc.vector.scalar_tensor_tensor(gen_rel[:], gen_dst[:, 1:2].to_broadcast([P, gen_k]), -1.0,
                                                   gen_off[:], ALU.add, ALU.subtract)
                    dve.wait_ge(g_gathered, 32 * (t + 1))
                    dve.wait_ge(g_z, t + 1)
                    nc.vector.tensor_tensor(gen_z, ps[:, 0, 0:hidden], gen_b, ALU.add).then_inc(g_step, 1)
                    dve.wait_ge(g_step, 4 * t + 3)
                    nc.vector.tensor_tensor(gen_z, gen_z, gen_a, ALU.add).then_inc(g_step, 1)
                    dve.wait_ge(g_prod, t + 1)
                    nc.vector.tensor_tensor(gen_msg[:], ps[:, 2, 0:feat], b2_bc[:], ALU.add).then_inc(g_msg, 1)
                    dve.wait_ge(g_step, 4 * t + 4)
                    dve.sem_inc(waited)
                    with dve.Fori(0, rounds) as r:
                        k = t * rounds + r
                        nc.vector.tensor_tensor(gen_oh[:], iota_gen[:].unsqueeze(1).to_broadcast([P, gen_k, gen_cols]),
                                                gen_rel[:].unsqueeze(2).to_broadcast([P, gen_k, gen_cols]),
                                                ALU.is_equal).then_inc(g_hot, 1)
                        dve.wait_ge(g_hot, k + 1)
                        nc.vector.tensor_scalar(gen_rel[:], gen_rel[:], float(gen_k * gen_cols), None, ALU.subtract)
                        dve.wait_ge(g_sum, k + 1)
                        part = out_sb[:, ds(r * (gen_k * gen_cols), gen_k * gen_cols)].rearrange(
                            "p (k n) -> p k n", k=gen_k)
                        nc.vector.tensor_tensor(part, ps[0:feat, 3:3 + gen_k, 0:gen_cols], part, ALU.add).then_inc(g_acc, 1)
                        dve.wait_ge(g_acc, k + 1)
            with dve.Else():
                dve.nop()
            nc.vector.memset(gen_dst[:, 0:1], 0.0).then_inc(sums_complete, 1)

        @block.tensor
        def _(pe):
            def turn_h(c, u, first):
                pe.wait_ge(h_ready, c + 1)
                if not first:
                    pe.wait_ge(ht_ready, c * units + u - (1 if u == 0 else 2) + 1)
                pe.sem_inc(waited)
                for j in range(2):
                    mm = nc.tensor.transpose(ps_ht[:, u % 2, j * P:(j + 1) * P], h_sb[:, 2 * u + j, :], ident[:])
                mm.then_inc(h_turned, 1)

            def products(c, u, first):
                pe.wait_ge(ht_ready, c * units + u + 1)
                if not first or u >= 3:
                    pe.wait_ge(b_ready, c * units + u - prod_gap[u] + 1)
                for j in range(2):
                    mm = nc.tensor.matmul(ps_b[:, prod_slot[u], j, :], h_t[h_row:h_end, u, j * P:(j + 1) * P],
                                          w_b[h_row:h_end, :], start=True, stop=True)
                mm.then_inc(prod_ready, 1)

            pe.wait_ge(ident_ready, 1)
            for u in range(units):
                turn_h(0, u, u < 2)
            pe.wait_ge(w_in, 32)

            def chunk(c, first, more):
                for u in range(units):
                    products(c, u, first)
                    if more:
                        turn_h(c + 1, u, False)

            chunk(0, True, True)
            with pe.Fori(1, chunks - 1) as c:
                chunk(c, False, True)
            pe.wait_ge(ones_ready, 3)
            pe.wait_ge(base_ready, 1)
            half = (groups + 1) // 2
            for k in range(2):
                g0, g1 = k * half, min(groups, (k + 1) * half)
                mm = nc.tensor.matmul(ps_base[:, k, 0:g1 - g0], ones_row[:], base_f[:, g0:g1], start=True, stop=True)
            mm.then_inc(base_spread, 1)
            chunk(chunks - 1, False, False)

            pe.wait_ge(inside_step, 2)
            nc.tensor.matmul(ps_sum[0:1, 0:1], covered[:], ones_col[:], start=True, stop=True).then_inc(cov_summed, 1)

            pe.wait_ge(we_in, 32 * SLOTS)
            pe.wait_ge(w2_in, 32)
            pe.wait_ge(b_ready, chunks * units)
            pe.wait_ge(flag_ready, 1)

            def turn_hot(s, u, first, fills):
                pe.wait_ge(hot_ready, s + 1)
                pe.wait_ge(win_loaded[u], 16 * fills)
                if not first:
                    pe.wait_ge(lhs_ready, s)
                pe.sem_inc(waited)
                nc.tensor.matmul(ps_aw, h_win[h_row:h_end, u, :], w_a[h_row:h_end, :], start=True, stop=True)
                for t in range(TILES):
                    mm = nc.tensor.transpose(ps_oht[:, t * P:(t + 1) * P], onehot[:, u, t, :], ident[:])
                mm.then_inc(hot_turned, 1)

            def gap(u):
                return (1, 3, 2, 2, 2)[u]

            def make_z(s, u, first, fills):
                pe.wait_ge(lhs_ready, s + 1)
                pe.wait_ge(loaded[u], 16 * fills)
                if not first:
                    pe.wait_ge(z_added, s - gap(u) + 1)
                for t in range(TILES):
                    mm = nc.tensor.matmul(ps_z[:, u % 2, t * P:(t + 1) * P], lhs[:, u, t * P:(t + 1) * P],
                                          rhs[:, u, :], start=True, stop=True)
                mm.then_inc(z_ready, 1)

            def make_sums(s, u):
                pe.wait_ge(r_ready, s + 1)
                for t in range(TILES):
                    mm = nc.tensor.matmul(ps_sum, gath[:, u, t, :], onehot[:, u, t, :],
                                          start=(t == 0), stop=(t == TILES - 1))
                mm.then_inc(summed, 1)

            def fold(s, u, first):
                pe.wait_ge(sums_copied, s + 1)
                if not first:
                    pe.wait_ge(out_added, s)
                for t in range(TILES):
                    nc.tensor.matmul(ps_out, b2_bc[:], onehot[:, u, t, :], start=(t == 0), stop=False)
                nc.tensor.matmul(ps_out, w2_sb[:], sums[:], start=False, stop=True).then_inc(folded, 1)

            for s in range(SLOTS):
                if s >= 4:
                    fold(s - 4, s - 4, True)
                if s >= 3:
                    make_sums(s - 3, s - 3)
                turn_hot(s, s, s == 0, 1)
                if s >= 1:
                    make_z(s - 1, s - 1, s - 1 < 2, 1)
            with pe.Fori(1, bodies) as it:
                for u in range(SLOTS):
                    s = it * SLOTS + u
                    fold(s - 4, (u - 4) % SLOTS, False)
                    make_sums(s - 3, (u - 3) % SLOTS)
                    turn_hot(s, u, False, it + 1)
                    make_z(s - 1, (u - 1) % SLOTS, False, it + 1 if u >= 1 else it)
            fold(groups - 4, SLOTS - 4, False)
            make_sums(groups - 3, SLOTS - 3)
            make_z(groups - 1, SLOTS - 1, False, bodies)
            for u in range(SLOTS - 3, SLOTS - 1):
                fold(groups - SLOTS + u, u, False)
                make_sums(groups - SLOTS + u + 1, u + 1)
            fold(groups - 1, SLOTS - 1, False)

            outside = pe.value_load(flag[0:1, 0:1], min_val=0, max_val=n_edges)
            with pe.If(outside > 0):
                with pe.Fori(0, node_tiles) as j:
                    pe.wait_ge(t_h, j + 1)
                    nc.tensor.matmul(ps[:, 0, 0:hidden], h_t[h_row:h_end, 0, 0:P], w_a[h_row:h_end, :],
                                     start=True, stop=True).then_inc(t_prod, 1)
                pe.wait_ge(t_out, node_tiles)
                with pe.Fori(0, n_tiles) as t:
                    pe.wait_ge(g_e_in, 16 * (t + 1))
                    nc.tensor.matmul(ps[:, 0, 0:hidden], lhs[e_row:k_rows, 1, 0:P], rhs[e_row:k_rows, 0, :],
                                     start=True, stop=True).then_inc(g_z, 1)
                    pe.wait_ge(g_r, t + 1)
                    nc.tensor.transpose(ps[:, 1, 0:P], gen_z, ident[:]).then_inc(g_turned, 1)
                    pe.wait_ge(g_rt, t + 1)
                    nc.tensor.matmul(ps[:, 2, 0:feat], gen_zt, w2_sb[:], start=True, stop=True).then_inc(g_prod, 1)
                    pe.wait_ge(g_msg, t + 1)
                    pe.sem_inc(waited)
                    with pe.Fori(0, rounds) as r:
                        pe.wait_ge(g_hot, t * rounds + r + 1)
                        for k in range(gen_k):
                            mm = nc.tensor.matmul(ps[0:feat, 3 + k, 0:gen_cols], gen_msg[:], gen_oh[:, k, :],
                                                  start=True, stop=True)
                        mm.then_inc(g_sum, 1)
            with pe.Else():
                pe.nop()


_INS = ["x_main", "x_last", "x_t", "src_t", "dst_t", "edge_t", "w1", "b1", "w2", "b2"]


def layouts(x, src, dst, edge, w1, b1, w2, b2):
    import numpy as np

    x = np.asarray(x)
    main = x.shape[0] // P * P
    return [np.ascontiguousarray(a) for a in (
        x[:main].reshape(-1, P, x.shape[1]).transpose(1, 0, 2), x[main:], x.T,
        np.asarray(src).reshape(-1, P).T, np.asarray(dst).reshape(-1, P).T, np.asarray(edge).T,
        np.asarray(w1), np.asarray(b1).reshape(1, -1), np.asarray(w2), np.asarray(b2))]


def kernel(x, src, dst, edge_attr_32, L0_gnn_W1, L0_gnn_b1, L0_gnn_W2, L0_gnn_b2):
    import numpy as np
    from concourse import bacc
    from concourse.bass_utils import run_bass_kernel_spmd

    given = layouts(x, src, dst, edge_attr_32, L0_gnn_W1, L0_gnn_b1, L0_gnn_W2, L0_gnn_b2)
    nc = bacc.Bacc("TRN2", target_bir_lowering=False, num_devices=1)
    arrays, args = {}, []
    for name, a in zip(_INS, given):
        arrays[f"in_{name}"] = a
        args.append(nc.dram_tensor(f"in_{name}", a.shape, mybir.dt.from_np(a.dtype), kind="ExternalInput").ap())
    out = nc.dram_tensor("out_t", given[2].shape, F32, kind="ExternalOutput").ap()
    gnn(nc, *args, out)
    r = run_bass_kernel_spmd(nc, [arrays], core_ids=[0])
    return np.ascontiguousarray(r.results[0]["out_t"].T)
```

```python
from contextlib import ExitStack

import concourse.bass as bass
from concourse import mybir

F32 = mybir.dt.float32
I32 = mybir.dt.int32
ALU = mybir.AluOpType
ACT = mybir.ActivationFunctionType
AX = mybir.AxisListType
ds = bass.ds

P = 128
BANK = 512
TILES = 5
SLOTS = 5
WIN = 64
EPS = 1e-5


def gnn(nc, x_main, x_last, x_t, src_t, dst_t, edge_t, w1, b1, w2, b2, out_t):
    feat, n_nodes = x_t.shape
    edge_feat, n_edges = edge_t.shape
    hidden = w1.shape[1]
    n_tiles = n_edges // P
    groups = n_tiles // TILES
    bodies = groups // SLOTS
    full = n_nodes // P
    last = n_nodes - full * P
    node_tiles = full + 1
    padded = node_tiles * P
    chunk_tiles, units = 14, 7
    chunks = node_tiles // chunk_tiles
    e_cols = TILES * P
    e_row = WIN
    one_row = e_row + edge_feat
    k_rows = one_row + 1
    h_row = 64
    h_end = h_row + feat
    early = SLOTS * TILES
    late = max(1, groups // 25)
    front = n_nodes * 7 // 8
    gen_cols, gen_k = 500, 5
    rounds = n_nodes // (gen_cols * gen_k)
    assert hidden == P and 0 < last < P and feat <= h_row and h_end <= P
    assert chunks * chunk_tiles == node_tiles and chunk_tiles == 2 * units and chunks % 2
    assert n_tiles * P == n_edges and bodies * SLOTS * TILES == n_tiles and bodies >= 2
    assert rounds * gen_cols * gen_k == n_nodes

    a_table = nc.dram_tensor("a_table", [padded, hidden], F32).ap()
    b_table = nc.dram_tensor("b_table", [padded, hidden], F32).ap()

    ctx = ExitStack()
    with ctx:
        def sb(name, shape, dt=F32):
            return ctx.enter_context(nc.sbuf_tensor(name, shape, dt))

        def sem(name):
            return ctx.enter_context(nc.semaphore(name))

        nodes = sb("nodes", [h_end, padded])
        src_sb = sb("src_sb", [P, n_tiles], I32)
        dst_sb = sb("dst_sb", [P, n_tiles], I32)
        dst_rel = sb("dst_rel", [P, n_tiles])
        gath = sb("gath", [P, SLOTS, TILES, hidden])
        lhs = sb("lhs", [k_rows, SLOTS, e_cols])
        rhs = sb("rhs", [k_rows, SLOTS, hidden])
        onehot = sb("onehot", [P, SLOTS, TILES, WIN])
        h_win = sb("h_win", [h_end, SLOTS, WIN])
        sums = sb("sums", [P, WIN])
        idx = sb("idx", [P, SLOTS, TILES], I32)
        x_sb = sb("x_sb", [P, node_tiles, feat])
        h_sb = sb("h_sb", [P, 2, chunk_tiles, h_row])
        sq_sb = sb("sq_sb", [P, chunk_tiles, feat])
        stat = sb("stat", [P, 5, chunk_tiles])
        h_t = sb("h_t", [h_end, units, P])
        b_stage = sb("b_stage", [P, units, 2, hidden])
        w_b = sb("w_b", [h_end, 2, hidden])
        w_a = sb("w_a", [h_end, hidden])
        w2_sb = sb("w2_sb", [hidden, feat])
        b2_bc = sb("b2_bc", [P, feat])
        ident = sb("ident", [P, P])
        ones_row = sb("ones_row", [1, P])
        ones_col = sb("ones_col", [P, 1])
        iota_gen = sb("iota_gen", [P, gen_cols])
        base_f = sb("base_f", [1, groups])
        base_i = sb("base_i", [1, groups], I32)
        covered = sb("covered", [P, 1])
        flag = sb("flag", [1, 1], I32)
        late_min = sb("late_min", [1, 2])
        settled = sb("settled", [1, 1], I32)
        gen_idx = sb("gen_idx", [P, 2], I32)
        gen_dst = sb("gen_dst", [P, 2])
        gen_rel = sb("gen_rel", [P, gen_k])
        gen_off = sb("gen_off", [P, gen_k])
        gen_oh = sb("gen_oh", [P, gen_k, gen_cols])
        gen_msg = sb("gen_msg", [P, feat])

        out_sb = nodes[0:feat, 0:n_nodes]
        h_all = nodes[h_row:h_end, :]
        inside = dst_sb[:].bitcast(F32)
        gen_z = gath[:, 0, 0, :]
        gen_b = gath[:, 1, 0, :]
        gen_a = gath[:, 2, 0, :]
        gen_zt = gath[:, 3, 0, :]

        ps = ctx.enter_context(nc.psum_tensor("ps", [P, 8, BANK], F32))
        ps_b = ps[:, 0:3, 0:2 * hidden].rearrange("p s (j w) -> p s j w", j=2)
        ps_ht = ps[0:h_end, 3:6, 0:P]
        ps_base = ps[:, 6:8, :]
        ps_z = ps[:, 0:4, :].rearrange("p (s b) c -> p s (b c)", b=2)[:, :, 0:e_cols]
        ps_win = ps[0:WIN, 4:6, :].rearrange("p b c -> p (b c)")
        ps_oht = ps_win[:, 0:e_cols]
        ps_aw = ps_win[:, 2 * BANK - hidden:2 * BANK]
        ps_sum = ps[:, 6, 0:WIN]
        ps_out = ps[0:feat, 6, WIN:2 * WIN]
        ps_last = ps[0:feat, 3, 0:WIN]
        iota_ps = ps[:, 7, 0:WIN]

        stores = ((0, 3), (3, 6), (6, 7))
        store_of = [k for k, (u0, u1) in enumerate(stores) for _ in range(u0, u1)]
        assert stores[-1][1] == units

        x_first, x_second, x_rest = sem("x_first"), sem("x_second"), sem("x_rest")
        x_tail, xt_in, pads_zero = sem("x_tail"), sem("xt_in"), sem("pads_zero")
        w_in, we_in, w2_in = sem("w_in"), sem("we_in"), sem("w2_in")
        dst_in, src_early, src_in = sem("dst_in"), sem("src_early"), sem("src_in")
        tail_zero, ident_zero, ident_ready = sem("tail_zero"), sem("ident_zero"), sem("ident_ready")
        ones_ready, iota_ready, iota_copied = sem("ones_ready"), sem("iota_ready"), sem("iota_copied")
        base_ready, base_spread, rel_ready, inside_step = sem("base_ready"), sem("base_spread"), sem("rel_ready"), sem("inside_step")
        cov_summed, flag_ready = sem("cov_summed"), sem("flag_ready")
        settled_step, settled_ready = sem("settled_step"), sem("settled_ready")
        stat_step, var_ready, std_ready, rstd_ready = sem("stat_step"), sem("var_ready"), sem("std_ready"), sem("rstd_ready")
        h_ready, h_turned, ht_ready, odd_kept = sem("h_ready"), sem("h_turned"), sem("ht_ready"), sem("odd_kept")
        even_kept = sem("even_kept")
        prod_ready, b_ready = sem("prod_ready"), sem("b_ready")
        b_stored = [sem(f"b_stored{k}") for k in range(len(stores))]
        idx_ready, hot_ready, hot_turned, lhs_ready = sem("idx_ready"), sem("hot_ready"), sem("hot_turned"), sem("lhs_ready")
        gathered = [sem(f"gathered{u}") for u in range(SLOTS)]
        loaded = [sem(f"loaded{u}") for u in range(SLOTS)]
        win_loaded = [sem(f"win_loaded{u}") for u in range(SLOTS)]
        z_ready, z_added, r_ready = sem("z_ready"), sem("z_added"), sem("r_ready")
        summed, sums_copied, folded, out_added = sem("summed"), sem("sums_copied"), sem("folded"), sem("out_added")
        out_stored = sem("out_stored")
        t_h, t_prod, t_out, t_stored = sem("t_h"), sem("t_prod"), sem("t_out"), sem("t_stored")
        g_idx_in, g_e_in, g_gathered = sem("g_idx_in"), sem("g_e_in"), sem("g_gathered")
        g_z, g_step, g_r, g_turned, g_rt = sem("g_z"), sem("g_step"), sem("g_r"), sem("g_turned"), sem("g_rt")
        g_prod, g_msg, g_hot, g_sum, g_acc = sem("g_prod"), sem("g_msg"), sem("g_hot"), sem("g_sum"), sem("g_acc")

        b_rows = b_table.rearrange("(j p) h -> p j h", p=P)

        pair_slot = (0, 1, 2, 0, 1, 2, 1)
        pair_gap = (4, 2, 4, 3, 3, 3, 2)

        waited = sem("waited")

        block = ctx.enter_context(nc.Block())

        @block.sync
        def _(sp):
            sp.dma_start(x_sb[:, 0:chunk_tiles, :], x_main[:, 0:chunk_tiles, :]).then_inc(x_first, 16)
            sp.dma_start(x_sb[:, chunk_tiles:2 * chunk_tiles, :], x_main[:, chunk_tiles:2 * chunk_tiles, :]
                         ).then_inc(x_second, 16)
            sp.dma_start(x_sb[:, 2 * chunk_tiles:full, :], x_main[:, 2 * chunk_tiles:full, :]).then_inc(x_rest, 16)
            sp.wait_ge(pads_zero, 1)
            sp.dma_start(w_b[0:feat, 0, :], w1[feat:2 * feat, :]).then_inc(w_in, 16)
            sp.dma_start(w_b[h_row:h_end, 1, :], w1[feat:2 * feat, :]).then_inc(w_in, 16)
            sp.wait_ge(tail_zero, 1)
            sp.dma_start(x_sb[0:last, full, :], x_last).then_inc(x_tail, 16)
            sp.dma_start(dst_sb[:], dst_t).then_inc(dst_in, 16)
            sp.dma_start(src_sb[:, 0:early], src_t[:, 0:early]).then_inc(src_early, 16)
            sp.dma_start(w_a[h_row:h_end, :], w1[0:feat, :]).then_inc(we_in, 16)
            for s in range(SLOTS):
                sp.dma_start(rhs[e_row:one_row, s, :], w1[2 * feat:2 * feat + edge_feat, :]).then_inc(we_in, 16)
                sp.dma_start(rhs[one_row:k_rows, s, :], b1).then_inc(we_in, 16)
            sp.dma_start(w2_sb[:], w2).then_inc(w2_in, 16)
            sp.dma_start(b2_bc[:], b2.partition_broadcast(P)).then_inc(w2_in, 16)

            with sp.Fori(0, chunks) as c:
                for k, (u0, u1) in enumerate(stores):
                    sp.wait_ge(b_ready, c * units + u1)
                    sp.dma_start(b_rows[:, ds(c * chunk_tiles + 2 * u0, 2 * (u1 - u0)), :],
                                 b_stage[:, u0:u1, :, :].rearrange("p u j w -> p (u j) w")).then_inc(b_stored[k], 16)

            sp.wait_ge(base_ready, 2)
            sp.wait_ge(odd_kept, chunks * units)
            sp.wait_ge(even_kept, chunks * units)

            def load_group(s, u, first):
                if not first:
                    sp.wait_ge(z_ready, s - SLOTS + 1)
                sp.dma_start(lhs[e_row:one_row, u, :], edge_t[:, ds(s * e_cols, e_cols)]).then_inc(loaded[u], 16)
                base = sp.value_load(base_i[0:1, ds(s, 1)], min_val=0, max_val=n_nodes - WIN)
                sp.dma_start(h_win[h_row:h_end, u, :], h_all[:, ds(base, WIN)]).then_inc(win_loaded[u], 16)

            for u in range(SLOTS):
                load_group(u, u, True)
            sp.dma_start(src_sb[:, early:n_tiles], src_t[:, early:n_tiles]).then_inc(src_in, 16)
            sp.dma_start(out_sb, x_t).then_inc(xt_in, 16)
            with sp.Fori(1, bodies) as it:
                for u in range(SLOTS):
                    load_group(it * SLOTS + u, u, False)

            sp.wait_ge(settled_ready, 1)
            front_settled = sp.value_load(settled[0:1, 0:1], min_val=0, max_val=1)
            with sp.If(front_settled > 0):
                sp.wait_ge(out_added, groups - late)
                sp.dma_start(out_t[:, 0:front], out_sb[:, 0:front]).then_inc(out_stored, 16)
            with sp.Else():
                sp.nop()

            sp.wait_ge(flag_ready, 1)
            outside = sp.value_load(flag[0:1, 0:1], min_val=0, max_val=n_edges)
            with sp.If(outside > 0):
                with sp.Fori(0, node_tiles) as j:
                    sp.wait_ge(t_out, j + 1)
                    sp.dma_start(a_table[ds(j * P, P), :], gen_a).then_inc(t_stored, 16)

                def load_tile(t):
                    sp.dma_start(gen_idx[:, 0:1], src_t[:, ds(t, 1)], allow_slow_non_contiguous=True).then_inc(g_idx_in, 16)
                    sp.dma_start(gen_idx[:, 1:2], dst_t[:, ds(t, 1)], allow_slow_non_contiguous=True).then_inc(g_idx_in, 16)
                    sp.dma_start(lhs[e_row:one_row, 1, 0:P], edge_t[:, ds(t * P, P)]).then_inc(g_e_in, 16)

                load_tile(0)
                with sp.Fori(1, n_tiles) as t:
                    sp.wait_ge(g_acc, t * rounds)
                    sp.sem_inc(waited)
                    load_tile(t)
                sp.wait_ge(g_acc, n_tiles * rounds)
            with sp.Else():
                sp.wait_ge(out_added, groups)
            sp.dma_start(out_t[:, front:n_nodes], out_sb[:, front:n_nodes]).then_inc(out_stored, 16)
            with sp.If(front_settled < 1):
                sp.dma_start(out_t[:, 0:front], out_sb[:, 0:front]).then_inc(out_stored, 16)
            with sp.Else():
                sp.nop()
            sp.wait_ge(out_stored, 32)

        @block.gpsimd
        def _(pool):
            nc.gpsimd.memset(x_sb[:, full, :], 0.0).then_inc(tail_zero, 1)
            nc.gpsimd.memset(ident[:], 0.0).then_inc(ident_zero, 1)
            pool.wait_ge(ident_zero, 1)
            nc.gpsimd.affine_select(out=ident[:], in_=ident[:], compare_op=ALU.not_equal, fill=1.0, base=0,
                                    pattern=[[-1, P]], channel_multiplier=1).then_inc(ident_ready, 1)
            nc.gpsimd.memset(ones_row[:], 1.0).then_inc(ones_ready, 1)
            nc.gpsimd.memset(ones_col[:], 1.0).then_inc(ones_ready, 1)
            pool.wait_ge(ones_ready, 2)
            nc.gpsimd.memset(lhs[one_row:k_rows, :, :], 1.0).then_inc(ones_ready, 1)
            pool.wait_ge(ones_ready, 3)
            nc.gpsimd.iota(iota_gen[:], [[1, gen_cols]], base=0, channel_multiplier=0,
                           allow_small_or_imprecise_dtypes=True).then_inc(iota_ready, 1)
            nc.gpsimd.iota(gen_off[:], [[gen_cols, gen_k]], base=0, channel_multiplier=0,
                           allow_small_or_imprecise_dtypes=True).then_inc(iota_ready, 1)

            pool.wait_ge(iota_ready, 2)
            with pool.Fori(0, chunks) as c:
                for u in range(units):
                    pool.wait_ge(ht_ready, c * units + u + 1)
                    nc.gpsimd.tensor_copy(h_all[:, ds(c * (chunk_tiles * P) + (2 * u + 1) * P, P)],
                                          h_t[h_row:h_end, u, :]).then_inc(odd_kept, 1)

            pool.wait_ge(odd_kept, chunks * units)
            for k in range(len(stores)):
                pool.wait_ge(b_stored[k], 16 * chunks)

            def gather_group(s, u):
                pool.wait_ge(idx_ready, s + 1)
                pool.sem_inc(waited)
                for t in range(TILES):
                    pool.indirect_dma_start(
                        gath[:, u, t, :], None, b_table,
                        bass.IndirectOffsetOnAxis(ap=idx[:, u, t:t + 1], axis=0)).then_inc(gathered[u], 16)

            for u in range(SLOTS):
                gather_group(u, u)
            with pool.Fori(1, bodies) as it:
                for u in range(SLOTS):
                    gather_group(it * SLOTS + u, u)

            outside = pool.value_load(flag[0:1, 0:1], min_val=0, max_val=n_edges)
            with pool.If(outside > 0):
                pool.wait_ge(t_stored, 16 * node_tiles)
                with pool.Fori(0, n_tiles) as t:
                    pool.wait_ge(g_idx_in, 32 * (t + 1))
                    pool.sem_inc(waited)
                    pool.indirect_dma_start(gen_b, None, b_table, bass.IndirectOffsetOnAxis(
                        ap=gen_idx[:, 0:1], axis=0)).then_inc(g_gathered, 16)
                    pool.indirect_dma_start(gen_a, None, a_table, bass.IndirectOffsetOnAxis(
                        ap=gen_idx[:, 1:2], axis=0)).then_inc(g_gathered, 16)
            with pool.Else():
                pool.nop()

        @block.scalar
        def _(act):
            def root(c):
                act.wait_ge(var_ready, c + 1)
                nc.scalar.activation(stat[:, 3, :], stat[:, 2, :], ACT.Sqrt).then_inc(std_ready, 1)

            def take_ht(c, u, first):
                act.wait_ge(h_turned, c * units + u + 1)
                if not first:
                    act.wait_ge(odd_kept, (c - 1) * units + u + 1)
                nc.scalar.copy(h_t[:, u, :], ps_ht[:, pair_slot[u], :]).then_inc(ht_ready, 1)
                nc.scalar.copy(h_all[:, ds(c * (chunk_tiles * P) + 2 * u * P, P)], ps_ht[0:feat, pair_slot[u], :]
                               ).then_inc(even_kept, 1)

            def take_b(c, u, first):
                act.wait_ge(prod_ready, c * units + u + 1)
                if not first:
                    act.wait_ge(b_stored[store_of[u]], 16 * c)
                nc.scalar.copy(b_stage[:, u, :, :], ps_b[:, pair_slot[u], :, :]).then_inc(b_ready, 1)

            root(0)
            for u in range(units):
                take_ht(0, u, True)
            root(1)

            def chunk(c, first, ht, stats):
                for u in range(units):
                    take_b(c, u, first)
                    if ht:
                        take_ht(c + 1, u, False)
                    if stats and u == 3:
                        root(c + 2)

            chunk(0, True, True, True)
            with act.Fori(1, chunks - 2) as c:
                chunk(c, False, True, True)
            chunk(chunks - 2, False, True, False)
            act.wait_ge(src_early, 16)

            def take_idx(s, u, first):
                if not first:
                    act.wait_ge(summed, s - SLOTS + 1)
                nc.scalar.copy(idx[:, u, :], src_sb[:, ds(s * TILES, TILES)]).then_inc(idx_ready, 1)

            take_idx(0, 0, True)
            take_idx(1, 1, True)
            chunk(chunks - 1, False, False, False)
            act.wait_ge(iota_ready, 2)
            act.wait_ge(rel_ready, 2)
            nc.scalar.copy(iota_ps, iota_gen[:, 0:WIN]).then_inc(iota_copied, 1)

            def take_hot(s, u, first):
                act.wait_ge(hot_turned, s + 1)
                if not first:
                    act.wait_ge(z_ready, s - SLOTS + 1)
                nc.scalar.copy(rhs[0:WIN, u, :], ps_aw)
                nc.scalar.copy(lhs[0:WIN, u, :], ps_oht).then_inc(lhs_ready, 1)

            def rectify(s, u):
                act.wait_ge(z_added, s + 1)
                z = gath[:, u, :, :]
                nc.scalar.activation(z, z, ACT.Relu).then_inc(r_ready, 1)

            for s in range(SLOTS):
                if s >= 2:
                    take_idx(s, s, True)
                take_hot(s, s, True)
                if s >= 2:
                    rectify(s - 2, s - 2)
            act.wait_ge(src_in, 16)
            with act.Fori(1, bodies) as it:
                for u in range(SLOTS):
                    s = it * SLOTS + u
                    take_idx(s, u, False)
                    take_hot(s, u, False)
                    rectify(s - 2, (u - 2) % SLOTS)
            rectify(groups - 2, SLOTS - 2)
            rectify(groups - 1, SLOTS - 1)

            outside = act.value_load(flag[0:1, 0:1], min_val=0, max_val=n_edges)
            with act.If(outside > 0):
                def take_tile(j):
                    nc.scalar.copy(h_t[h_row:h_end, 0, 0:P], h_all[:, ds(j * P, P)]).then_inc(t_h, 1)

                take_tile(0)
                with act.Fori(1, node_tiles) as j:
                    act.wait_ge(t_stored, 16 * j)
                    take_tile(j)
                with act.Fori(0, n_tiles) as t:
                    act.wait_ge(g_step, 4 * t + 4)
                    nc.scalar.activation(gen_z, gen_z, ACT.Relu).then_inc(g_r, 1)
                    act.wait_ge(g_turned, t + 1)
                    nc.scalar.copy(gen_zt, ps[:, 1, 0:P]).then_inc(g_rt, 1)
            with act.Else():
                act.nop()

        @block.vector
        def _(dve):
            def stats(c, chained):
                xc = x_sb[:, ds(c * chunk_tiles, chunk_tiles), :]
                nc.vector.tensor_reduce(stat[:, 0, :], xc, AX.X, ALU.add).then_inc(stat_step, 1)
                dve.wait_ge(stat_step, 4 * c + 1)
                nc.vector.scalar_tensor_tensor(
                    xc, stat[:, 0, :].unsqueeze(2).to_broadcast([P, chunk_tiles, feat]), -1.0 / feat, xc,
                    ALU.mult, ALU.add).then_inc(stat_step, 1)
                dve.wait_ge(stat_step, 4 * c + 2)
                nc.vector.tensor_tensor(sq_sb[:], xc, xc, ALU.mult).then_inc(stat_step, 1)
                dve.wait_ge(stat_step, 4 * c + 3)
                nc.vector.tensor_reduce(stat[:, 1, :], sq_sb[:], AX.X, ALU.add).then_inc(stat_step, 1)
                dve.wait_ge(stat_step, 4 * c + 4)
                nc.vector.tensor_scalar(stat[:, 2, :], stat[:, 1, :], 1.0 / feat, EPS, ALU.mult, ALU.add
                                        ).then_inc(var_ready, 1)
                dve.wait_ge(std_ready, c + 1)
                if chained:
                    dve.wait_ge(h_ready, c)
                nc.vector.reciprocal(stat[:, 4, :], stat[:, 3, :]).then_inc(rstd_ready, 1)

            def write_h(c, half, first):
                dve.wait_ge(rstd_ready, c + 1)
                if not first:
                    dve.wait_ge(h_turned, (c - 1) * units)
                nc.vector.scalar_tensor_tensor(
                    h_sb[:, half, :, 0:feat], x_sb[:, ds(c * chunk_tiles, chunk_tiles), :], 0.0,
                    stat[:, 4, :].unsqueeze(2).to_broadcast([P, chunk_tiles, feat]),
                    ALU.max, ALU.mult).then_inc(h_ready, 1)

            nc.vector.memset(w_b[:], 0.0).then_inc(pads_zero, 1)
            nc.vector.memset(h_sb[:], 0.0).then_inc(pads_zero, 1)
            dve.wait_ge(x_first, 16)
            stats(0, False)
            dve.wait_ge(pads_zero, 2)
            write_h(0, 0, True)
            dve.wait_ge(x_second, 16)
            stats(1, True)
            write_h(1, 1, True)
            dve.wait_ge(x_rest, 16)
            dve.wait_ge(x_tail, 16)
            with dve.Fori(1, chunks // 2) as two:
                for half in range(2):
                    stats(two * 2 + half, True)
                    write_h(two * 2 + half, half, False)
            stats(chunks - 1, True)
            write_h(chunks - 1, 0, False)

            dve.wait_ge(dst_in, 16)
            firsts = dst_sb[0:1, :].rearrange("p (g t) -> p g t", t=TILES)[:, :, 0]
            nc.vector.tensor_scalar(base_f[:], firsts, float(n_nodes - WIN), None, ALU.min).then_inc(base_ready, 1)
            nc.vector.tensor_scalar(base_i[:], firsts, float(n_nodes - WIN), None, ALU.min).then_inc(base_ready, 1)
            dve.wait_ge(base_spread, 1)
            half = (groups + 1) // 2
            for k in range(2):
                g0, g1 = k * half, min(groups, (k + 1) * half)
                nc.vector.tensor_tensor(
                    dst_rel[:, g0 * TILES:g1 * TILES].rearrange("p (g t) -> p g t", t=TILES),
                    dst_sb[:, g0 * TILES:g1 * TILES].rearrange("p (g t) -> p g t", t=TILES),
                    ps_base[:, k, 0:g1 - g0].unsqueeze(2).to_broadcast([P, g1 - g0, TILES]),
                    ALU.subtract).then_inc(rel_ready, 1)
            dve.wait_ge(rel_ready, 2)
            nc.vector.tensor_scalar(inside, dst_rel[:], 0.0, None, ALU.is_ge).then_inc(inside_step, 1)
            dve.wait_ge(inside_step, 1)
            nc.vector.scalar_tensor_tensor(inside, dst_rel[:], float(WIN), inside, ALU.is_lt, ALU.mult,
                                           accum_out=covered[:]).then_inc(inside_step, 1)
            dve.wait_ge(cov_summed, 1)
            nc.vector.tensor_scalar(flag[:], ps_sum[0:1, 0:1], -1.0, float(n_edges), ALU.mult, ALU.add
                                    ).then_inc(flag_ready, 1)
            nc.vector.tensor_reduce(late_min[:, 0:1], base_f[:, groups - late:groups], AX.X, ALU.min
                                    ).then_inc(settled_step, 1)
            dve.wait_ge(settled_step, 1)
            nc.vector.tensor_scalar(late_min[:, 1:2], late_min[:, 0:1], float(front), None, ALU.is_ge
                                    ).then_inc(settled_step, 1)
            dve.wait_ge(settled_step, 2)
            dve.wait_ge(flag_ready, 1)
            nc.vector.scalar_tensor_tensor(settled[:], flag[:], 0.0, late_min[:, 1:2], ALU.is_equal, ALU.mult
                                           ).then_inc(settled_ready, 1)
            dve.wait_ge(iota_copied, 1)

            def make_hot(s, u, first):
                if not first:
                    dve.wait_ge(folded, s - SLOTS + 1)
                nc.vector.tensor_tensor(
                    onehot[:, u, :, :], iota_ps.unsqueeze(1).to_broadcast([P, TILES, WIN]),
                    dst_rel[:, ds(s * TILES, TILES)].unsqueeze(2).to_broadcast([P, TILES, WIN]),
                    ALU.is_equal).then_inc(hot_ready, 1)

            def add_z(s, u, fills):
                dve.wait_ge(z_ready, s + 1)
                dve.wait_ge(gathered[u], 16 * TILES * fills)
                z = gath[:, u, :, :].rearrange("p t h -> p (t h)")
                nc.vector.tensor_tensor(z, ps_z[:, u % 2, :], z, ALU.add).then_inc(z_added, 1)

            def copy_sums(s):
                dve.wait_ge(summed, s + 1)
                nc.vector.tensor_copy(sums[:], ps_sum).then_inc(sums_copied, 1)

            def add_out(s, first, alone=False, part=ps_out):
                dve.wait_ge(folded, s + 1)
                if not alone:
                    dve.wait_ge(summed, s + 2)
                if not first:
                    dve.wait_ge(out_added, s)
                base = dve.value_load(base_i[0:1, ds(s, 1)], min_val=0, max_val=n_nodes - WIN)
                nc.vector.tensor_tensor(out_sb[:, ds(base, WIN)], part, out_sb[:, ds(base, WIN)], ALU.add
                                        ).then_inc(out_added, 1)

            for s in range(SLOTS):
                make_hot(s, s, True)
                if s >= 2:
                    add_z(s - 2, s - 2, 1)
                if s >= 4:
                    dve.wait_ge(xt_in, 16)
                    add_out(s - 4, True)
                if s >= 3:
                    copy_sums(s - 3)
            with dve.Fori(1, bodies) as it:
                for u in range(SLOTS):
                    s = it * SLOTS + u
                    make_hot(s, u, False)
                    add_z(s - 2, (u - 2) % SLOTS, it + 1 if u >= 2 else it)
                    add_out(s - 4, False)
                    copy_sums(s - 3)
            add_z(groups - 2, SLOTS - 2, bodies)
            for s in range(groups - 4, groups - 2):
                add_out(s, False)
                copy_sums(s + 1)
            add_z(groups - 1, SLOTS - 1, bodies)
            add_out(groups - 2, False, alone=True)
            copy_sums(groups - 1)
            add_out(groups - 1, False, alone=True, part=ps_last)

            outside = dve.value_load(flag[0:1, 0:1], min_val=0, max_val=n_edges)
            with dve.If(outside > 0):
                with dve.Fori(0, node_tiles) as j:
                    dve.wait_ge(t_prod, j + 1)
                    nc.vector.tensor_copy(gen_a, ps[:, 0, 0:hidden]).then_inc(t_out, 1)
                with dve.Fori(0, n_tiles) as t:
                    dve.wait_ge(g_idx_in, 32 * (t + 1))
                    nc.vector.tensor_scalar(gen_dst[:, 0:1], inside[:, ds(t, 1)], -1.0, 1.0, ALU.mult, ALU.add
                                            ).then_inc(g_step, 1)
                    dve.wait_ge(g_step, 4 * t + 1)
                    nc.vector.scalar_tensor_tensor(gen_dst[:, 1:2], gen_idx[:, 1:2], 1.0, gen_dst[:, 0:1],
                                                   ALU.add, ALU.mult).then_inc(g_step, 1)
                    dve.wait_ge(g_step, 4 * t + 2)
                    nc.vector.scalar_tensor_tensor(gen_rel[:], gen_dst[:, 1:2].to_broadcast([P, gen_k]), -1.0,
                                                   gen_off[:], ALU.add, ALU.subtract)
                    dve.wait_ge(g_gathered, 32 * (t + 1))
                    dve.wait_ge(g_z, t + 1)
                    nc.vector.tensor_tensor(gen_z, ps[:, 0, 0:hidden], gen_b, ALU.add).then_inc(g_step, 1)
                    dve.wait_ge(g_step, 4 * t + 3)
                    nc.vector.tensor_tensor(gen_z, gen_z, gen_a, ALU.add).then_inc(g_step, 1)
                    dve.wait_ge(g_prod, t + 1)
                    nc.vector.tensor_tensor(gen_msg[:], ps[:, 2, 0:feat], b2_bc[:], ALU.add).then_inc(g_msg, 1)
                    dve.wait_ge(g_step, 4 * t + 4)
                    dve.sem_inc(waited)
                    with dve.Fori(0, rounds) as r:
                        k = t * rounds + r
                        nc.vector.tensor_tensor(gen_oh[:], iota_gen[:].unsqueeze(1).to_broadcast([P, gen_k, gen_cols]),
                                                gen_rel[:].unsqueeze(2).to_broadcast([P, gen_k, gen_cols]),
                                                ALU.is_equal).then_inc(g_hot, 1)
                        dve.wait_ge(g_hot, k + 1)
                        nc.vector.tensor_scalar(gen_rel[:], gen_rel[:], float(gen_k * gen_cols), None, ALU.subtract)
                        dve.wait_ge(g_sum, k + 1)
                        part = out_sb[:, ds(r * (gen_k * gen_cols), gen_k * gen_cols)].rearrange(
                            "p (k n) -> p k n", k=gen_k)
                        nc.vector.tensor_tensor(part, ps[0:feat, 3:3 + gen_k, 0:gen_cols], part, ALU.add).then_inc(g_acc, 1)
                        dve.wait_ge(g_acc, k + 1)
            with dve.Else():
                dve.nop()

        @block.tensor
        def _(pe):
            def turn_h(c, half, u, first):
                pe.wait_ge(h_ready, c + 1)
                if not first:
                    pe.wait_ge(even_kept, c * units + u - pair_gap[u] + 1)
                pe.sem_inc(waited)
                nc.tensor.transpose(ps_ht[:, pair_slot[u], :],
                                    h_sb[:, half, 2 * u:2 * u + 2, :].rearrange("p j f -> p (j f)")[:, 0:h_end],
                                    ident[:]).then_inc(h_turned, 1)

            def products(c, u, first):
                pe.wait_ge(ht_ready, c * units + u + 1)
                if not first or u >= 3:
                    pe.wait_ge(b_ready, c * units + u - pair_gap[u] + 1)
                nc.tensor.matmul(ps_b[:, pair_slot[u], :, :].rearrange("p j w -> p (j w)"), h_t[:, u, :],
                                 w_b[:].rearrange("p j w -> p (j w)"), start=True, stop=True).then_inc(prod_ready, 1)

            pe.wait_ge(ident_ready, 1)
            for u in range(units):
                turn_h(0, 0, u, u < 3)
            pe.wait_ge(w_in, 32)

            def chunk(c, half, first, more):
                for u in range(units):
                    products(c, u, first)
                    if more:
                        turn_h(c + 1, half, u, False)

            chunk(0, 1, True, True)
            with pe.Fori(0, chunks // 2 - 1) as two:
                for half in range(2):
                    chunk(two * 2 + half + 1, half, False, True)
            chunk(chunks - 2, 0, False, True)
            pe.wait_ge(ones_ready, 3)
            pe.wait_ge(base_ready, 1)
            half = (groups + 1) // 2
            for k in range(2):
                g0, g1 = k * half, min(groups, (k + 1) * half)
                mm = nc.tensor.matmul(ps_base[:, k, 0:g1 - g0], ones_row[:], base_f[:, g0:g1], start=True, stop=True)
            mm.then_inc(base_spread, 1)
            chunk(chunks - 1, 1, False, False)

            pe.wait_ge(inside_step, 2)
            nc.tensor.matmul(ps_sum[0:1, 0:1], covered[:], ones_col[:], start=True, stop=True).then_inc(cov_summed, 1)

            pe.wait_ge(we_in, 32 * SLOTS + 16)
            pe.wait_ge(w2_in, 32)
            pe.wait_ge(b_ready, chunks * units)
            pe.wait_ge(flag_ready, 1)

            def turn_hot(s, u, first, fills):
                pe.wait_ge(hot_ready, s + 1)
                pe.wait_ge(win_loaded[u], 16 * fills)
                if not first:
                    pe.wait_ge(lhs_ready, s)
                pe.sem_inc(waited)
                nc.tensor.matmul(ps_aw, h_win[h_row:h_end, u, :], w_a[h_row:h_end, :], start=True, stop=True)
                for t in range(TILES):
                    mm = nc.tensor.transpose(ps_oht[:, t * P:(t + 1) * P], onehot[:, u, t, :], ident[:])
                mm.then_inc(hot_turned, 1)

            def gap(u):
                return (1, 3, 2, 2, 2)[u]

            def make_z(s, u, first, fills):
                pe.wait_ge(lhs_ready, s + 1)
                pe.wait_ge(loaded[u], 16 * fills)
                if not first:
                    pe.wait_ge(z_added, s - gap(u) + 1)
                for t in range(TILES):
                    mm = nc.tensor.matmul(ps_z[:, u % 2, t * P:(t + 1) * P], lhs[:, u, t * P:(t + 1) * P],
                                          rhs[:, u, :], start=True, stop=True)
                mm.then_inc(z_ready, 1)

            def make_sums(s, u):
                pe.wait_ge(r_ready, s + 1)
                for t in range(TILES):
                    mm = nc.tensor.matmul(ps_sum, gath[:, u, t, :], onehot[:, u, t, :],
                                          start=(t == 0), stop=(t == TILES - 1))
                mm.then_inc(summed, 1)

            def fold_b2(u, to):
                for t in range(TILES):
                    nc.tensor.matmul(to, b2_bc[:], onehot[:, u, t, :], start=(t == 0), stop=False)

            def fold(s, u, first):
                pe.wait_ge(sums_copied, s + 1)
                if not first:
                    pe.wait_ge(out_added, s)
                fold_b2(u, ps_out)
                nc.tensor.matmul(ps_out, w2_sb[:], sums[:], start=False, stop=True).then_inc(folded, 1)

            for s in range(SLOTS):
                if s >= 4:
                    fold(s - 4, s - 4, True)
                if s >= 3:
                    make_sums(s - 3, s - 3)
                turn_hot(s, s, s == 0, 1)
                if s >= 1:
                    make_z(s - 1, s - 1, s - 1 < 2, 1)
            with pe.Fori(1, bodies) as it:
                for u in range(SLOTS):
                    s = it * SLOTS + u
                    fold(s - 4, (u - 4) % SLOTS, False)
                    make_sums(s - 3, (u - 3) % SLOTS)
                    turn_hot(s, u, False, it + 1)
                    make_z(s - 1, (u - 1) % SLOTS, False, it + 1 if u >= 1 else it)
            fold(groups - 4, SLOTS - 4, False)
            make_sums(groups - 3, SLOTS - 3)
            make_z(groups - 1, SLOTS - 1, False, bodies)
            fold(groups - 3, SLOTS - 3, False)
            make_sums(groups - 2, SLOTS - 2)
            fold(groups - 2, SLOTS - 2, False)
            pe.wait_ge(z_added, groups - 1)
            fold_b2(SLOTS - 1, ps_last)
            pe.wait_ge(out_added, groups - 1)
            make_sums(groups - 1, SLOTS - 1)
            pe.wait_ge(sums_copied, groups)
            nc.tensor.matmul(ps_last, w2_sb[:], sums[:], start=False, stop=True).then_inc(folded, 1)

            outside = pe.value_load(flag[0:1, 0:1], min_val=0, max_val=n_edges)
            with pe.If(outside > 0):
                with pe.Fori(0, node_tiles) as j:
                    pe.wait_ge(t_h, j + 1)
                    nc.tensor.matmul(ps[:, 0, 0:hidden], h_t[h_row:h_end, 0, 0:P], w_a[h_row:h_end, :],
                                     start=True, stop=True).then_inc(t_prod, 1)
                pe.wait_ge(t_out, node_tiles)
                with pe.Fori(0, n_tiles) as t:
                    pe.wait_ge(g_e_in, 16 * (t + 1))
                    nc.tensor.matmul(ps[:, 0, 0:hidden], lhs[e_row:k_rows, 1, 0:P], rhs[e_row:k_rows, 0, :],
                                     start=True, stop=True).then_inc(g_z, 1)
                    pe.wait_ge(g_r, t + 1)
                    nc.tensor.transpose(ps[:, 1, 0:P], gen_z, ident[:]).then_inc(g_turned, 1)
                    pe.wait_ge(g_rt, t + 1)
                    nc.tensor.matmul(ps[:, 2, 0:feat], gen_zt, w2_sb[:], start=True, stop=True).then_inc(g_prod, 1)
                    pe.wait_ge(g_msg, t + 1)
                    pe.sem_inc(waited)
                    with pe.Fori(0, rounds) as r:
                        pe.wait_ge(g_hot, t * rounds + r + 1)
                        for k in range(gen_k):
                            mm = nc.tensor.matmul(ps[0:feat, 3 + k, 0:gen_cols], gen_msg[:], gen_oh[:, k, :],
                                                  start=True, stop=True)
                        mm.then_inc(g_sum, 1)
            with pe.Else():
                pe.nop()


_INS = ["x_main", "x_last", "x_t", "src_t", "dst_t", "edge_t", "w1", "b1", "w2", "b2"]


def layouts(x, src, dst, edge, w1, b1, w2, b2):
    import numpy as np

    x = np.asarray(x)
    main = x.shape[0] // P * P
    return [np.ascontiguousarray(a) for a in (
        x[:main].reshape(-1, P, x.shape[1]).transpose(1, 0, 2), x[main:], x.T,
        np.asarray(src).reshape(-1, P).T, np.asarray(dst).reshape(-1, P).T, np.asarray(edge).T,
        np.asarray(w1), np.asarray(b1).reshape(1, -1), np.asarray(w2), np.asarray(b2))]


def kernel(x, src, dst, edge_attr_32, L0_gnn_W1, L0_gnn_b1, L0_gnn_W2, L0_gnn_b2):
    import numpy as np
    from concourse import bacc
    from concourse.bass_utils import run_bass_kernel_spmd

    given = layouts(x, src, dst, edge_attr_32, L0_gnn_W1, L0_gnn_b1, L0_gnn_W2, L0_gnn_b2)
    nc = bacc.Bacc("TRN2", target_bir_lowering=False, num_devices=1)
    arrays, args = {}, []
    for name, a in zip(_INS, given):
        arrays[f"in_{name}"] = a
        args.append(nc.dram_tensor(f"in_{name}", a.shape, mybir.dt.from_np(a.dtype), kind="ExternalInput").ap())
    out = nc.dram_tensor("out_t", given[2].shape, F32, kind="ExternalOutput").ap()
    gnn(nc, *args, out)
    r = run_bass_kernel_spmd(nc, [arrays], core_ids=[0])
    return np.ascontiguousarray(r.results[0]["out_t"].T)
```
